# Optimizing a Trainium2 kernel written in Bass

```python
import numpy as np
import jax
import jax.numpy as jnp

def _softmax(x, axis=-1):
    return jax.nn.softmax(x, axis=axis)

def _gelu(x):
    return jax.nn.gelu(x, approximate=True)

def _silu(x):
    return jax.nn.silu(x)

def _sigmoid(x):
    return jax.nn.sigmoid(x)

def _layernorm(x, axis=-1, eps=1e-05):
    m = jnp.mean(x, axis=axis, keepdims=True)
    v = jnp.var(x, axis=axis, keepdims=True)
    return (x - m) / jnp.sqrt(v + eps)

def _scatter_add(tgt, idx, src, axis=0):
    return tgt.at[idx].add(src)

def _segment_sum(src, seg, n):
    return jax.ops.segment_sum(src, seg, n)
kernel_name = 'mk_dlrm_tower_d1_rec_r8_d115a5'

def setup_inputs(seed: int=0):
    np.random.seed(seed)
    _w = jnp.asarray

    def _rec_inputs():
        import jax
        import jax.numpy as jnp
        _tk = jax.random.key(seed)
        dense_ctx = jax.random.normal(jax.random.fold_in(_tk, 190), (2048, 16), jnp.float32)
        ids = jnp.stack([jax.random.randint(jax.random.fold_in(_tk, 200 + f), (2048,), 0, v, jnp.int32) for f, v in enumerate([125000, 1250, 1250, 1000, 125000, 1250, 1000, 1000, 1000, 12500, 1000, 125000, 12500, 12500, 125000, 125000, 1000, 12500, 125000, 125000, 1250, 1000, 1000, 1000, 12500, 12500, 12500, 12500, 125000, 1000, 1250, 125000, 125000, 1000, 125000, 125000, 125000, 125000, 12500])], axis=1)
        tbl_0 = 0.05 * jax.random.normal(jax.random.fold_in(_tk, 500 + 0), (125000, 16), jnp.float32)
        tbl_1 = 0.05 * jax.random.normal(jax.random.fold_in(_tk, 500 + 1), (1250, 16), jnp.float32)
        tbl_2 = 0.05 * jax.random.normal(jax.random.fold_in(_tk, 500 + 2), (1250, 16), jnp.float32)
        tbl_3 = 0.05 * jax.random.normal(jax.random.fold_in(_tk, 500 + 3), (1000, 16), jnp.float32)
        tbl_4 = 0.05 * jax.random.normal(jax.random.fold_in(_tk, 500 + 4), (125000, 16), jnp.float32)
        tbl_5 = 0.05 * jax.random.normal(jax.random.fold_in(_tk, 500 + 5), (1250, 16), jnp.float32)
        tbl_6 = 0.05 * jax.random.normal(jax.random.fold_in(_tk, 500 + 6), (1000, 16), jnp.float32)
        tbl_7 = 0.05 * jax.random.normal(jax.random.fold_in(_tk, 500 + 7), (1000, 16), jnp.float32)
        tbl_8 = 0.05 * jax.random.normal(jax.random.fold_in(_tk, 500 + 8), (1000, 16), jnp.float32)
        tbl_9 = 0.05 * jax.random.normal(jax.random.fold_in(_tk, 500 + 9), (12500, 16), jnp.float32)
        tbl_10 = 0.05 * jax.random.normal(jax.random.fold_in(_tk, 500 + 10), (1000, 16), jnp.float32)
        tbl_11 = 0.05 * jax.random.normal(jax.random.fold_in(_tk, 500 + 11), (125000, 16), jnp.float32)
        tbl_12 = 0.05 * jax.random.normal(jax.random.fold_in(_tk, 500 + 12), (12500, 16), jnp.float32)
        tbl_13 = 0.05 * jax.random.normal(jax.random.fold_in(_tk, 500 + 13), (12500, 16), jnp.float32)
        tbl_14 = 0.05 * jax.random.normal(jax.random.fold_in(_tk, 500 + 14), (125000, 16), jnp.float32)
        tbl_15 = 0.05 * jax.random.normal(jax.random.fold_in(_tk, 500 + 15), (125000, 16), jnp.float32)
        tbl_16 = 0.05 * jax.random.normal(jax.random.fold_in(_tk, 500 + 16), (1000, 16), jnp.float32)
        tbl_17 = 0.05 * jax.random.normal(jax.random.fold_in(_tk, 500 + 17), (12500, 16), jnp.float32)
        tbl_18 = 0.05 * jax.random.normal(jax.random.fold_in(_tk, 500 + 18), (125000, 16), jnp.float32)
        tbl_19 = 0.05 * jax.random.normal(jax.random.fold_in(_tk, 500 + 19), (125000, 16), jnp.float32)
        tbl_20 = 0.05 * jax.random.normal(jax.random.fold_in(_tk, 500 + 20), (1250, 16), jnp.float32)
        tbl_21 = 0.05 * jax.random.normal(jax.random.fold_in(_tk, 500 + 21), (1000, 16), jnp.float32)
        tbl_22 = 0.05 * jax.random.normal(jax.random.fold_in(_tk, 500 + 22), (1000, 16), jnp.float32)
        tbl_23 = 0.05 * jax.random.normal(jax.random.fold_in(_tk, 500 + 23), (1000, 16), jnp.float32)
        tbl_24 = 0.05 * jax.random.normal(jax.random.fold_in(_tk, 500 + 24), (12500, 16), jnp.float32)
        tbl_25 = 0.05 * jax.random.normal(jax.random.fold_in(_tk, 500 + 25), (12500, 16), jnp.float32)
        tbl_26 = 0.05 * jax.random.normal(jax.random.fold_in(_tk, 500 + 26), (12500, 16), jnp.float32)
        tbl_27 = 0.05 * jax.random.normal(jax.random.fold_in(_tk, 500 + 27), (12500, 16), jnp.float32)
        tbl_28 = 0.05 * jax.random.normal(jax.random.fold_in(_tk, 500 + 28), (125000, 16), jnp.float32)
        tbl_29 = 0.05 * jax.random.normal(jax.random.fold_in(_tk, 500 + 29), (1000, 16), jnp.float32)
        tbl_30 = 0.05 * jax.random.normal(jax.random.fold_in(_tk, 500 + 30), (1250, 16), jnp.float32)
        tbl_31 = 0.05 * jax.random.normal(jax.random.fold_in(_tk, 500 + 31), (125000, 16), jnp.float32)
        tbl_32 = 0.05 * jax.random.normal(jax.random.fold_in(_tk, 500 + 32), (125000, 16), jnp.float32)
        tbl_33 = 0.05 * jax.random.normal(jax.random.fold_in(_tk, 500 + 33), (1000, 16), jnp.float32)
        tbl_34 = 0.05 * jax.random.normal(jax.random.fold_in(_tk, 500 + 34), (125000, 16), jnp.float32)
        tbl_35 = 0.05 * jax.random.normal(jax.random.fold_in(_tk, 500 + 35), (125000, 16), jnp.float32)
        tbl_36 = 0.05 * jax.random.normal(jax.random.fold_in(_tk, 500 + 36), (125000, 16), jnp.float32)
        tbl_37 = 0.05 * jax.random.normal(jax.random.fold_in(_tk, 500 + 37), (125000, 16), jnp.float32)
        tbl_38 = 0.05 * jax.random.normal(jax.random.fold_in(_tk, 500 + 38), (12500, 16), jnp.float32)
        _rk = jax.random.fold_in(_tk, 7)
        W_top1 = 0.0693375 * jax.random.normal(jax.random.fold_in(_tk, 801), (208, 512), jnp.float32)
        W_top2 = 0.0441942 * jax.random.normal(jax.random.fold_in(_tk, 802), (512, 256), jnp.float32)
        W_top3 = 0.0625 * jax.random.normal(jax.random.fold_in(_tk, 803), (256, 1), jnp.float32)
        b_top1 = jnp.zeros((512,), jnp.float32)
        b_top2 = jnp.zeros((256,), jnp.float32)
        return (dense_ctx, ids, tbl_0, tbl_1, tbl_2, tbl_3, tbl_4, tbl_5, tbl_6, tbl_7, tbl_8, tbl_9, tbl_10, tbl_11, tbl_12, tbl_13, tbl_14, tbl_15, tbl_16, tbl_17, tbl_18, tbl_19, tbl_20, tbl_21, tbl_22, tbl_23, tbl_24, tbl_25, tbl_26, tbl_27, tbl_28, tbl_29, tbl_30, tbl_31, tbl_32, tbl_33, tbl_34, tbl_35, tbl_36, tbl_37, tbl_38, W_top1, b_top1, W_top2, b_top2, W_top3)
    dense_ctx, ids, tbl_0, tbl_1, tbl_2, tbl_3, tbl_4, tbl_5, tbl_6, tbl_7, tbl_8, tbl_9, tbl_10, tbl_11, tbl_12, tbl_13, tbl_14, tbl_15, tbl_16, tbl_17, tbl_18, tbl_19, tbl_20, tbl_21, tbl_22, tbl_23, tbl_24, tbl_25, tbl_26, tbl_27, tbl_28, tbl_29, tbl_30, tbl_31, tbl_32, tbl_33, tbl_34, tbl_35, tbl_36, tbl_37, tbl_38, W_top1, b_top1, W_top2, b_top2, W_top3 = _rec_inputs()

    def _L0_rec_setup():
        import jax, jax.numpy as jnp
        import numpy as np
        B, F, D = (512, 39, 16)
        L0, L1 = (128, 128)
        H1 = L0 // 2

        def _cin_layer(h, h0, W, b):
            z = jnp.einsum('bhd,bmd->bhmd', h, h0)
            z = z.reshape(z.shape[0], -1, z.shape[-1])
            y = jnp.einsum('oc,bcd->bod', W, z) + b[None, :, None]
            return jax.nn.relu(y)
        key = jax.random.key(seed)
        k0, k1, k2, k3, k4 = jax.random.split(key, 5)
        x = jax.random.normal(k0, (B, F, D), dtype=jnp.float32)
        W0 = jax.random.normal(k1, (L0, F * F), dtype=jnp.float32) * 0.02
        b0 = jnp.zeros((L0,), dtype=jnp.float32)
        W1 = jax.random.normal(k2, (L1, H1 * F), dtype=jnp.float32) * 0.02
        b1 = jnp.zeros((L1,), dtype=jnp.float32)
        return {'x': x, 'W0': W0, 'b0': b0, 'W1': W1, 'b1': b1}
    _L0_rec_all = _L0_rec_setup()
    _L0_rec_in = {k: v for k, v in _L0_rec_all.items() if k in ('W0', 'b0', 'W1', 'b1')}
    del _L0_rec_all
    return {'dense_ctx': dense_ctx, 'ids': ids, 'tbl_0': tbl_0, 'tbl_1': tbl_1, 'tbl_2': tbl_2, 'tbl_3': tbl_3, 'tbl_4': tbl_4, 'tbl_5': tbl_5, 'tbl_6': tbl_6, 'tbl_7': tbl_7, 'tbl_8': tbl_8, 'tbl_9': tbl_9, 'tbl_10': tbl_10, 'tbl_11': tbl_11, 'tbl_12': tbl_12, 'tbl_13': tbl_13, 'tbl_14': tbl_14, 'tbl_15': tbl_15, 'tbl_16': tbl_16, 'tbl_17': tbl_17, 'tbl_18': tbl_18, 'tbl_19': tbl_19, 'tbl_20': tbl_20, 'tbl_21': tbl_21, 'tbl_22': tbl_22, 'tbl_23': tbl_23, 'tbl_24': tbl_24, 'tbl_25': tbl_25, 'tbl_26': tbl_26, 'tbl_27': tbl_27, 'tbl_28': tbl_28, 'tbl_29': tbl_29, 'tbl_30': tbl_30, 'tbl_31': tbl_31, 'tbl_32': tbl_32, 'tbl_33': tbl_33, 'tbl_34': tbl_34, 'tbl_35': tbl_35, 'tbl_36': tbl_36, 'tbl_37': tbl_37, 'tbl_38': tbl_38, 'W_top1': W_top1, 'b_top1': b_top1, 'W_top2': W_top2, 'b_top2': b_top2, 'W_top3': W_top3, 'L0_rec_W0': _L0_rec_in['W0'], 'L0_rec_b0': _L0_rec_in['b0'], 'L0_rec_W1': _L0_rec_in['W1'], 'L0_rec_b1': _L0_rec_in['b1']}

def reference(dense_ctx, ids, tbl_0, tbl_1, tbl_2, tbl_3, tbl_4, tbl_5, tbl_6, tbl_7, tbl_8, tbl_9, tbl_10, tbl_11, tbl_12, tbl_13, tbl_14, tbl_15, tbl_16, tbl_17, tbl_18, tbl_19, tbl_20, tbl_21, tbl_22, tbl_23, tbl_24, tbl_25, tbl_26, tbl_27, tbl_28, tbl_29, tbl_30, tbl_31, tbl_32, tbl_33, tbl_34, tbl_35, tbl_36, tbl_37, tbl_38, W_top1, b_top1, W_top2, b_top2, W_top3, L0_rec_W0, L0_rec_b0, L0_rec_W1, L0_rec_b1):
    import jax
    import jax.numpy as jnp

    def _L0_rec_ref(x, W0, b0, W1, b1):
        import jax, jax.numpy as jnp
        import numpy as np
        B, F, D = (512, 39, 16)
        L0, L1 = (128, 128)
        H1 = L0 // 2

        def _cin_layer(h, h0, W, b):
            z = jnp.einsum('bhd,bmd->bhmd', h, h0)
            z = z.reshape(z.shape[0], -1, z.shape[-1])
            y = jnp.einsum('oc,bcd->bod', W, z) + b[None, :, None]
            return jax.nn.relu(y)
        h0 = x
        y0 = _cin_layer(h0, h0, W0, b0)
        next_hidden, direct0 = (y0[:, :H1, :], y0[:, H1:, :])
        direct1 = _cin_layer(next_hidden, h0, W1, b1)
        result = jnp.sum(jnp.concatenate([direct0, direct1], axis=1), axis=-1)
        return result
    e = jnp.stack([tbl_0[ids[:, 0]], tbl_1[ids[:, 1]], tbl_2[ids[:, 2]], tbl_3[ids[:, 3]], tbl_4[ids[:, 4]], tbl_5[ids[:, 5]], tbl_6[ids[:, 6]], tbl_7[ids[:, 7]], tbl_8[ids[:, 8]], tbl_9[ids[:, 9]], tbl_10[ids[:, 10]], tbl_11[ids[:, 11]], tbl_12[ids[:, 12]], tbl_13[ids[:, 13]], tbl_14[ids[:, 14]], tbl_15[ids[:, 15]], tbl_16[ids[:, 16]], tbl_17[ids[:, 17]], tbl_18[ids[:, 18]], tbl_19[ids[:, 19]], tbl_20[ids[:, 20]], tbl_21[ids[:, 21]], tbl_22[ids[:, 22]], tbl_23[ids[:, 23]], tbl_24[ids[:, 24]], tbl_25[ids[:, 25]], tbl_26[ids[:, 26]], tbl_27[ids[:, 27]], tbl_28[ids[:, 28]], tbl_29[ids[:, 29]], tbl_30[ids[:, 30]], tbl_31[ids[:, 31]], tbl_32[ids[:, 32]], tbl_33[ids[:, 33]], tbl_34[ids[:, 34]], tbl_35[ids[:, 35]], tbl_36[ids[:, 36]], tbl_37[ids[:, 37]], tbl_38[ids[:, 38]]], axis=1)
    z = _L0_rec_ref(e, L0_rec_W0, L0_rec_b0, L0_rec_W1, L0_rec_b1)
    z = z.reshape(z.shape[0], -1)
    h = jnp.concatenate([z, dense_ctx], axis=1)
    h = jnp.maximum(h @ W_top1 + b_top1, 0.0)
    h = jnp.maximum(h @ W_top2 + b_top2, 0.0)
    y = h @ W_top3
    return y

_drawn_inputs = setup_inputs


def setup_inputs(seed=0):
    import zlib

    import numpy as np

    out = dict(_drawn_inputs(seed))
    spreads = {'b_top1': (0.0, 0.8),
     'b_top2': (0.0, 0.35),
     'L0_rec_b0': (0.0, 0.1),
     'L0_rec_b1': (0.0, 0.1)}
    factors = {'tbl_0': 8.0,
     'tbl_1': 8.0,
     'tbl_2': 8.0,
     'tbl_3': 8.0,
     'tbl_4': 8.0,
     'tbl_5': 8.0,
     'tbl_6': 8.0,
     'tbl_7': 8.0,
     'tbl_8': 8.0,
     'tbl_9': 8.0,
     'tbl_10': 8.0,
     'tbl_11': 8.0,
     'tbl_12': 8.0,
     'tbl_13': 8.0,
     'tbl_14': 8.0,
     'tbl_15': 8.0,
     'tbl_16': 8.0,
     'tbl_17': 8.0,
     'tbl_18': 8.0,
     'tbl_19': 8.0,
     'tbl_20': 8.0,
     'tbl_21': 8.0,
     'tbl_22': 8.0,
     'tbl_23': 8.0,
     'tbl_24': 8.0,
     'tbl_25': 8.0,
     'tbl_26': 8.0,
     'tbl_27': 8.0,
     'tbl_28': 8.0,
     'tbl_29': 8.0,
     'tbl_30': 8.0,
     'tbl_31': 8.0,
     'tbl_32': 8.0,
     'tbl_33': 8.0,
     'tbl_34': 8.0,
     'tbl_35': 8.0,
     'tbl_36': 8.0,
     'tbl_37': 8.0,
     'tbl_38': 8.0,
     'L0_rec_W0': 8.0,
     'L0_rec_W1': 3.707}
    for name, (base, spread) in spreads.items():
        noise = np.random.default_rng([zlib.crc32(name.encode()), seed]).standard_normal(out[name].shape)
        drawn = base * np.exp(spread * noise) if base else spread * noise
        out[name] = jnp.asarray(drawn.astype(out[name].dtype))
    for name, factor in factors.items():
        out[name] = (out[name] * factor).astype(out[name].dtype)
    return out
```

```python
from contextlib import ExitStack

import numpy as np
import concourse.bass as bass
from concourse import mybir

F32 = mybir.dt.float32
F32R = mybir.dt.float32r
BF16 = mybir.dt.bfloat16
I32 = mybir.dt.int32
ALU = mybir.AluOpType
ACT = mybir.ActivationFunctionType
AX_X = mybir.AxisListType.X

B, F, D = 2048, 39, 16
P = 128
BT = B // P
DG = 4
G = D // DG
NT = BT * G
C = DG * P
H0 = 64
PARTS = 3
KX = PARTS * F
NPAIR = F * (F - 1) // 2
NSQ = NPAIR + F
Q_FULL = NSQ // P
Q_REST = NSQ - Q_FULL * P
NQ = Q_FULL + 1
NP1 = (F + 1) // 2
N1, N2, DENSE = 512, 256, 16

ORDER = [("q", 0), ("q", 1), ("p", 0), ("p", 1), ("p", 2), ("q", 2), ("p", 3), ("p", 4), ("q", 3),
         ("p", 5), ("p", 6), ("p", 7), ("x", 0), ("p", 8), ("p", 9)]
HEAD = [("x", 0), ("x", 1), ("q", 0), ("q", 1), ("q", 2), ("q", 3)]
J, JH = len(ORDER), len(HEAD)
LAG = 4
NB = 3
NZ = 6
assert J * G % NB == 0 and J * G % NZ == 0 and JH % NB == 0 and JH % NZ == 0
QJ = [n for n, j in enumerate(ORDER) if j[0] == "q"]
PJ = [n for n, j in enumerate(ORDER) if j[0] == "p"]
XJ = ORDER.index(("x", 0))
GATHER_AT = list(range(13))
assert len(GATHER_AT) * 3 == F
SPLIT_AT = 5
Y0_AT = QJ[-1] + LAG + 1
Y1_AT = LAG


def lo_on_pool(r, job):
    return job in ([("p", 1), ("p", 5), ("p", 8)] if r != 2 else
                   [("q", 1), ("p", 1), ("p", 3), ("q", 3), ("p", 6), ("p", 8)])


GATHER_AFTER = ("p", 8)
assert lo_on_pool(2, GATHER_AFTER)


def t_has_gathers(t):
    return not isinstance(t, int) or t < NT - 7


def lo_count(r, pool, upto=J):
    return sum(1 for j in ORDER[:upto] if j[0] != "x" and lo_on_pool(r, j) == pool)


def kind_count(kind, upto=J):
    return sum(1 for j in ORDER[:upto] if j[0] == kind)


LO_POOL = [lo_count(r, True) for r in range(G)]
LO_DVE = [lo_count(r, False) for r in range(G)]
ZJ = J - 1
ZH_ = JH - 2

def exists(t, kind):
    return not isinstance(t, int) or t < NT - {"p": 0, "q": 1, "x": 2}[kind]


def missing(t, n, kinds, chosen=lambda job: True):
    if not isinstance(t, int):
        return 0
    return sum(1 for u in range(NT - 2, t + 1) for j in ORDER[:n + 1 if u == t else J]
               if j[0] in kinds and not exists(u, j[0]) and chosen(j))


def bcast_done(t, n):
    if n < 0:
        return bcast_done(t - 1, n + J)
    return t * J + (JH + n + 1 - missing(t, n, "qx"))


def main_done(t, n):
    if n < 0:
        return main_done(t - 1, n + J)
    return t * ZJ + (ZH_ + n + 1 - kind_count("x", n + 1) - missing(t, n, "q"))


def prods_done(t, n):
    if n < 0:
        return prods_done(t - 1, n + J)
    return t * (NP1 // 2) + kind_count("p", n + 1)


hi_done = main_done


def lo_done(t, bt, r, n, pool):
    each = LO_POOL if pool else LO_DVE
    base = 0 if pool else ZH_
    lack = missing(t, n, "q", lambda job: lo_on_pool(G - 1, job) == pool)
    return bt * sum(each) + (base + sum(each[:r]) + lo_count(r, pool, n + 1) - lack)


def pair_runs():
    at, out = 0, []
    for h in range(F - 1):
        out.append((h, at))
        at += F - 1 - h
    return out


def selections():
    sel = np.zeros((F, (NQ + NP1) * P), np.float32)
    for h, at in pair_runs():
        for m in range(h + 1, F):
            sel[h, at + m - h - 1] = sel[m, at + m - h - 1] = 1
    for h in range(F):
        sel[h, NPAIR + h] = 1
    rest = sel[:, Q_FULL * P:NSQ].copy()
    sel[:, NSQ:NSQ + Q_REST] = rest
    for k in range(NP1):
        for j in range(2):
            sel[min(2 * k + j, F - 1), (NQ + k) * P + j * H0:(NQ + k) * P + (j + 1) * H0] = 1
    return np.tile(sel, (PARTS, 1))


def dlrm_cin_tower(nc, dense, ids, tables, wt1, bt1, wt2, bt2, wt3, w0, b0, w1, b1,
                   sel_d, identb_d, identf_d, out):
    with ExitStack() as ctx:
        def sb(name, shape, dt, where=ctx):
            return where.enter_context(nc.sbuf_tensor(name, shape, dt))

        def sem(name):
            return ctx.enter_context(nc.semaphore(name))

        sel = sb("sel", [KX, (NQ + NP1) * P], BF16)
        identb = sb("identb", [P, P], BF16)
        identf = sb("identf", [P, P], F32)
        idx = sb("idx", [P, F], I32)
        xg = sb("xg", [P, F, D], F32)
        res1 = sb("res1", [P, F, D], F32)
        res2 = sb("res2", [P, F, D], F32)
        xs = sb("xs", [P, PARTS, F, D], BF16)
        xt = sb("xt", [KX, 4, C], BF16)
        y2 = sb("y2", [P, 2, C], F32)
        qh = sb("qh", [P, NQ, P], F32R)
        ql = sb("ql", [P, NQ, P], F32R)
        ph = sb("ph", [P, NP1, P], F32R)
        pl = sb("pl", [P, NP1, P], F32R)
        acc0 = sb("acc0", [P, C], F32)
        acc1 = sb("acc1", [P, C], F32)
        tmp0 = sb("tmp0", [P, C // 2], F32)
        tmp1 = sb("tmp1", [P, C // 2], F32)
        bias0 = sb("bias0", [P, 1], F32)
        bias1 = sb("bias1", [P, 1], F32)
        nb0 = sb("nb0", [P, 1], F32)
        nb1 = sb("nb1", [P, 1], F32)
        db0 = sb("db0", [P, 1], F32)
        db1 = sb("db1", [P, 1], F32)
        hta = sb("hta", [P, B], F32)
        htb = sb("htb", [P, B], F32)
        wa = sb("wa", [P, N1], F32)
        wb = sb("wb", [P, N1], F32)
        w2s = sb("w2s", [P, N1 // P, N2], F32)
        w3s = sb("w3s", [P, N2 // P], F32)
        bt1s = sb("bt1s", [P, N1 // P], F32)
        bt2s = sb("bt2s", [P, N2 // P], F32)
        dn = sb("dn", [P, BT, DENSE], F32)
        h1 = sb("h1", [P, N1 // P, C], F32)
        h2 = sb("h2", [P, N2 // P, C], F32)
        ys = sb("ys", [1, B], F32)
        with ExitStack() as scratch:
            w0s = sb("w0s", [P, F * F], F32, scratch)
            w1s = sb("w1s", [P, H0 * F], F32, scratch)
            pk = sb("pk", [P, NQ * P], F32, scratch)
            rsum = sb("rsum", [P, 3, F], F32, scratch)
            pkh = sb("pkh", [P, NQ * P], F32R, scratch)
            pkl = sb("pkl", [P, NQ * P], F32R, scratch)
            w1h = sb("w1h", [P, F, H0], F32R, scratch)
            w1l = sb("w1l", [P, F, H0], F32R, scratch)
            lastp = sb("lastp", [P, 2, P], F32, scratch)
            lastq = sb("lastq", [P, 2, P], F32, scratch)
        z = sb("z", [P, NZ, 2 * C], F32)
        zh = sb("zh", [P, NZ, 2 * C], F32R)
        zl = sb("zl", [P, NZ, 2 * C], F32R)

        bb = ctx.enter_context(nc.psum_tensor("bb", [P, NB, 2 * C], F32))
        y0p = ctx.enter_context(nc.psum_tensor("y0p", [P, C], F32))
        y1p = ctx.enter_context(nc.psum_tensor("y1p", [P, C], F32))

        s_w0 = sem("s_w0")
        s_w1 = sem("s_w1")
        s_const = sem("s_const")
        s_small = sem("s_small")
        s_top = sem("s_top")
        s_ids = sem("s_ids")
        s_gather = sem("s_gather")
        s_prep = sem("s_prep")
        s_wsplit = sem("s_wsplit")
        s_turn = sem("s_turn")
        s_turned_a = sem("s_turned_a")
        s_turned_v = sem("s_turned_v")
        s_zero = sem("s_zero")
        s_bias = sem("s_bias")
        s_part = sem("s_part")
        s_res = sem("s_res")
        s_bcast = sem("s_bcast")
        s_xt = sem("s_xt")
        s_sq = sem("s_sq")
        s_prod = sem("s_prod")
        s_hi = sem("s_hi")
        s_lod = sem("s_lod")
        s_lop = sem("s_lop")
        s_main = sem("s_main")
        s_y2 = sem("s_y2")
        s_acc0 = sem("s_acc0")
        s_acc1 = sem("s_acc1")
        s_half0 = sem("s_half0")
        s_half1 = sem("s_half1")
        s_ht0 = sem("s_ht0")
        s_ht1 = sem("s_ht1")
        s_m1 = sem("s_m1")
        s_m2 = sem("s_m2")
        s_m3 = sem("s_m3")
        s_a1 = sem("s_a1")
        s_a2 = sem("s_a2")
        s_a3 = sem("s_a3")
        s_out = sem("s_out")

        w1v = w1s[:, :].rearrange("o (h m) -> o m h", h=H0)
        w0v = w0s[:, :].rearrange("o (h m) -> o h m", h=F)
        NTURN_Q = 2 * NQ
        turns = []
        for k in range(NP1 - 1):
            turns += [(w1h[:, 2 * k:2 * k + 2, :].rearrange("o m h -> o (m h)"), ph[:, k, :]), (w1l[:, 2 * k:2 * k + 2, :].rearrange("o m h -> o (m h)"), pl[:, k, :])]
        turns += [(lastp[:, 0, :], ph[:, NP1 - 1, :]), (lastp[:, 1, :], pl[:, NP1 - 1, :])]
        for c in range(NQ - 1):
            turns += [(pkh[:, c * P:(c + 1) * P], qh[:, c, :]), (pkl[:, c * P:(c + 1) * P], ql[:, c, :])]
        turns += [(lastq[:, 0, :], qh[:, NQ - 1, :]), (lastq[:, 1, :], ql[:, NQ - 1, :])]
        TG = 2 * C // P
        groups = [turns[i:i + TG] for i in range(0, len(turns), TG)]
        NG = len(groups)

        def chunks(job):
            kind, n = job
            if kind == "q":
                return [2 * n, 2 * n + 1] if n < Q_FULL // 2 else [NQ - 1]
            return [2 * n, 2 * n + 1]

        def wide(job):
            return len(chunks(job)) * C

        block = ctx.enter_context(nc.Block())

        @block.sync
        def _(sp):
            sp.dma_start(idx[:, :], ids[0:P, :]).then_inc(s_ids, 16)
            sp.dma_start(w1s[:, :], w1).then_inc(s_w1, 16)
            sp.dma_start(w0s[:, :], w0).then_inc(s_w0, 16)
            sp.dma_start(identf[:, :], identf_d).then_inc(s_const, 16)
            sp.dma_start(identb[:, :], identb_d).then_inc(s_const, 16)
            sp.dma_start(sel[:, :], sel_d).then_inc(s_const, 16)
            sp.dma_start(bias0[:, :], b0.rearrange("(p a) -> p a", a=1)).then_inc(s_small, 16)
            sp.dma_start(bias1[:, :], b1.rearrange("(p a) -> p a", a=1)).then_inc(s_small, 16)
            sp.dma_start(bt1s[:, :], bt1.rearrange("(k p) -> p k", p=P),
                         allow_slow_non_contiguous=True).then_inc(s_small, 16)
            sp.dma_start(bt2s[:, :], bt2.rearrange("(k p) -> p k", p=P),
                         allow_slow_non_contiguous=True).then_inc(s_small, 16)
            sp.dma_start(w3s[:, :], wt3.rearrange("(k p) a -> p (k a)", p=P),
                         allow_slow_non_contiguous=True).then_inc(s_small, 16)
            sp.dma_start(dn[:, :, :], dense.rearrange("(t p) n -> p t n", p=P)).then_inc(s_top, 16)
            sp.dma_start(wa[:, :], wt1[H0:H0 + P, :]).then_inc(s_top, 16)
            sp.dma_start(w2s[:, :, :], wt2.rearrange("(k p) n -> p k n", p=P)).then_inc(s_top, 16)
            sp.wait_ge(s_zero, 2)
            sp.dma_start(wb[H0:P, :], wt1[0:H0, :]).then_inc(s_top, 16)
            sp.dma_start(wb[0:DENSE, :], wt1[H0 + P:H0 + P + DENSE, :]).then_inc(s_top, 16)
            with sp.Fori(1, BT) as b:
                sp.wait_ge(s_gather, b * (16 * F))
                sp.dma_start(idx[:, :], ids[bass.ts(b, P), :]).then_inc(s_ids, 16)
            sp.wait_ge(s_a3, G)
            sp.dma_start(out.rearrange("b a -> a b"), ys[:, :]).then_inc(s_out, 16)
            sp.wait_ge(s_out, 16)

        @block.gpsimd
        def _(pool):
            def gather(f):
                pool.indirect_dma_start(xg[:, f, :], None, tables[f],
                                        bass.IndirectOffsetOnAxis(idx[:, f:f + 1], 0)).then_inc(s_gather, 16)

            def remainders(b):
                pool.wait_ge(s_part, b * 3 + 1)
                pool.tensor_tensor(res1[:, :, :], xg[:, :, :], xs[:, 0, :, :], ALU.subtract).then_inc(s_res, 1)
                pool.wait_ge(s_part, b * 3 + 2)
                pool.wait_ge(s_res, b * 2 + 1)
                pool.tensor_tensor(res2[:, :, :], res1[:, :, :], xs[:, 1, :, :], ALU.subtract).then_inc(s_res, 1)

            def slot(t, bt, r, more):
                for n, job in enumerate(ORDER):
                    if r != 2 and n in GATHER_AT and more:
                        gather((r + 1) % G * len(GATHER_AT) + GATHER_AT.index(n))
                    if r == 2 and n == SPLIT_AT and more:
                        remainders(bt + 1)
                    if job[0] != "x" and exists(t, job[0]) and lo_on_pool(r, job):
                        i = (JH + r * J + n) % NZ
                        w = wide(job)
                        if r == 2 and job == GATHER_AFTER and t_has_gathers(t):
                            pool.wait_ge(s_ids, bt * 16 + 48)
                            pool.wait_ge(s_res, bt * 2 + 4)
                        pool.wait_ge(s_hi, hi_done(t, n))
                        pool.tensor_tensor(zl[:, i, 0:w], z[:, i, 0:w], zh[:, i, 0:w].bitcast(F32),
                                           ALU.subtract).then_inc(s_lop, 1)

            pool.wait_ge(s_ids, 16)
            for f in range(F):
                gather(f)
            remainders(0)
            pool.wait_ge(s_ids, 32)
            pool.wait_ge(s_res, 2)
            for f in range(len(GATHER_AT)):
                gather(f)
            slot(0, 0, 0, True)
            with pool.Fori(0, BT - 2) as b:
                for r in (1, 2, 3):
                    slot(b * G + r, b, r, True)
                slot(b * G + G, b + 1, 0, True)
            for t in range(NT - 7, NT):
                slot(t, t // G, t % G, t < NT - 5)

        @block.scalar
        def _(act):
            def parts(b, last_turn):
                act.wait_ge(s_gather, b * (16 * F) + 16 * F)
                if last_turn is not None:
                    act.wait_ge(s_bcast, last_turn)
                act.activation(xs[:, 0, :, :], xg[:, :, :], ACT.Copy).then_inc(s_part, 1)
                act.wait_ge(s_res, b * 2 + 1)
                act.activation(xs[:, 1, :, :], res1[:, :, :], ACT.Copy).then_inc(s_part, 1)
                act.wait_ge(s_res, b * 2 + 2)
                act.activation(xs[:, 2, :, :], res2[:, :, :], ACT.Copy).then_inc(s_part, 1)

            def take_xt(i, u, ready):
                act.wait_ge(s_bcast, ready)
                act.activation(xt[:, u, :], bb[0:KX, i % NB, 0:C // 2].bitcast(BF16), ACT.Copy)\
                   .then_inc(s_xt, 1)

            def squares(i, w, ready):
                act.wait_ge(s_bcast, ready)
                act.activation(z[:, i % NZ, 0:w], bb[:, i % NB, 0:w], ACT.Square).then_inc(s_sq, 1)
                act.activation(zh[:, i % NZ, 0:w], bb[:, i % NB, 0:w], ACT.Square).then_inc(s_hi, 1)

            def hidden(t, before, u):
                act.wait_ge(s_main, before)
                act.activation(y2[0:H0, u, :], y0p[0:H0, :], ACT.Relu, bias=bias0[0:H0, :])
                act.activation(y2[H0:P, u, :], y0p[0:H0, :], ACT.Relu, bias=bias0[0:H0, :]).then_inc(s_y2, 1)

            def slot(t, bt, r, first=False):
                for n, job in enumerate(ORDER):
                    i = JH + r * J + n
                    if job[0] == "x" and exists(t, "x"):
                        take_xt(i, (r + 2) % 4, bcast_done(t, n))
                    if job[0] == "q" and exists(t, "q"):
                        act.wait_ge(s_main, ZH_ if first and n < NZ else main_done(t, n - NZ))
                        squares(i, wide(job), bcast_done(t, n))
                    if job[0] == "p":
                        w = wide(job)
                        act.wait_ge(s_prod, prods_done(t, n))
                        act.activation(zh[:, i % NZ, 0:w], z[:, i % NZ, 0:w], ACT.Copy).then_inc(s_hi, 1)
                    if r == 2 and n == SPLIT_AT and exists(t, "x"):
                        parts(bt + 1, bcast_done(t, XJ - J))
                    if n == Y0_AT and exists(t, "q"):
                        act.wait_ge(s_prod, prods_done(t, -1))
                        hidden(t, main_done(t, QJ[-1]), (r + 1) % 2)

            act.wait_ge(s_w1, 16)
            act.activation(w1h[:, :, :], w1v, ACT.Copy).then_inc(s_wsplit, 1)
            act.wait_ge(s_prep, 3)
            act.activation(pkh[:, :], pk[:, :], ACT.Copy, scale=0.5).then_inc(s_wsplit, 1)
            for g in range(0, NG, 2):
                act.wait_ge(s_turn, g + 1)
                for j, (_, dst) in enumerate(groups[g]):
                    last = act.activation(dst, bb[:, g % NB, j * P:(j + 1) * P], ACT.Copy)
                last.then_inc(s_turned_a, 1)
            parts(0, None)
            for n, job in enumerate(HEAD):
                if job[0] == "x":
                    take_xt(n, job[1], n + 1)
                else:
                    squares(n, wide(job), n + 1)
            hidden(-1, ZH_, 0)
            slot(0, 0, 0, first=True)
            with act.Fori(0, BT - 2) as b:
                for r in (1, 2, 3):
                    slot(b * G + r, b, r)
                slot(b * G + G, b + 1, 0)
            for t in range(NT - 7, NT):
                slot(t, t // G, t % G)
            for g in range(G):
                for k in range(N1 // P):
                    act.wait_ge(s_m1, g * (N1 // P) + k + 1)
                    if g and k == 0:
                        act.wait_ge(s_m2, g * (N2 // P))
                    act.activation(h1[:, k, :], bb[:, k % NB, 0:C], ACT.Relu, bias=bt1s[:, k:k + 1])\
                       .then_inc(s_a1, 1)
                for k in range(N2 // P):
                    act.wait_ge(s_m2, g * (N2 // P) + k + 1)
                    if g and k == 0:
                        act.wait_ge(s_m3, g)
                    act.activation(h2[:, k, :], bb[:, k, C:2 * C], ACT.Relu, bias=bt2s[:, k:k + 1])\
                       .then_inc(s_a2, 1)
                act.wait_ge(s_m3, g + 1)
                act.activation(ys[:, g * C:(g + 1) * C], y0p[0:1, :], ACT.Copy).then_inc(s_a3, 1)

        @block.vector
        def _(dve):
            def low(i, w, ready):
                dve.wait_ge(s_hi, ready)
                dve.tensor_tensor(zl[:, i % NZ, 0:w], z[:, i % NZ, 0:w], zh[:, i % NZ, 0:w].bitcast(F32),
                                  ALU.subtract).then_inc(s_lod, 1)

            def direct0(u, bt, r, ready):
                dve.wait_ge(s_main, ready)
                y = y0p[H0:P, :]
                if r == 0:
                    if not (isinstance(u, int) and u == 0):
                        dve.wait_ge(s_half0, bt + 1)
                    dve.tensor_scalar(acc0[H0:P, :], y, nb0[H0:P, :], None, ALU.max).then_inc(s_acc0, 1)
                else:
                    dve.wait_ge(s_acc0, u)
                    dve.scalar_tensor_tensor(out=acc0[H0:P, :], in0=y, scalar=nb0[H0:P, :],
                                             in1=acc0[H0:P, :], op0=ALU.max, op1=ALU.add).then_inc(s_acc0, 1)

            def direct1(u, bt, r, ready):
                dve.wait_ge(s_main, ready)
                if r == 0:
                    if not (isinstance(u, int) and u == 0):
                        dve.wait_ge(s_half1, bt + 1)
                    dve.tensor_scalar(acc1[:, :], y1p[:, :], nb1[:, :], None, ALU.max).then_inc(s_acc1, 1)
                else:
                    dve.wait_ge(s_acc1, u)
                    dve.scalar_tensor_tensor(out=acc1[:, :], in0=y1p[:, :], scalar=nb1[:, :],
                                             in1=acc1[:, :], op0=ALU.max, op1=ALU.add).then_inc(s_acc1, 1)

            def finish(bt, rows, acc, tmp, db, ht, s_acc, s_half, s_ht):
                dve.wait_ge(s_acc, bt * G + G)
                dve.wait_ge(s_ht, bt + 1)
                dve.tensor_tensor(tmp[rows, :], acc[rows, 0:C // 2], acc[rows, C // 2:C], ALU.add).then_inc(s_half, 1)
                dve.wait_ge(s_half, bt + 2)
                dve.scalar_tensor_tensor(out=ht[rows, bass.ts(bt, P)], in0=tmp[rows, 0:P], scalar=db[rows, :],
                                         in1=tmp[rows, P:2 * P], op0=ALU.add, op1=ALU.add).then_inc(s_ht, 1)

            lo, hi = slice(H0, P), slice(0, P)

            def slot(t, bt, r, first=False):
                for n, job in enumerate(ORDER):
                    i = JH + r * J + n
                    if job[0] == "p":
                        w = wide(job)
                        dve.wait_ge(s_bcast, bcast_done(t, n))
                        dve.wait_ge(s_main, ZH_ if first and n < NZ else main_done(t, n - NZ))
                        if job[1] == 0:
                            dve.wait_ge(s_y2, t + 1)
                        y = y2[:, r % 2, :]
                        for k in range(2):
                            last = dve.tensor_tensor(z[:, i % NZ, k * C:(k + 1) * C], bb[:, i % NB, k * C:(k + 1) * C],
                                                     y, ALU.mult)
                        last.then_inc(s_prod, 1)
                    if n > 0:
                        before = ORDER[n - 1]
                        if before[0] != "x" and exists(t, before[0]) and not lo_on_pool(r, before):
                            low(i - 1, wide(before), hi_done(t, n - 1))
                    if n == J - 1 and not lo_on_pool(r, job):
                        low(i, wide(job), hi_done(t, n))
                    if n == Y1_AT and not first:
                        direct1(t - 1, bt, (r - 1) % G, main_done(t, -1))
                        if r == 0:
                            finish(bt - 1, hi, acc1, tmp1, db1, hta, s_acc1, s_half1, s_ht1)
                    if n == Y0_AT and exists(t, "q"):
                        direct0(t + 1, bt + 1 if r == 3 else bt, (r + 1) % G, main_done(t, QJ[-1]))
                        if r == 2:
                            finish(bt, lo, acc0, tmp0, db0, htb, s_acc0, s_half0, s_ht0)

            dve.memset(htb[0:H0, :], 0.0).then_inc(s_zero, 1)
            dve.memset(wb[0:H0, :], 0.0).then_inc(s_zero, 1)
            dve.memset(pk[:, NSQ:NQ * P], 0.0).then_inc(s_zero, 1)
            dve.memset(lastp[:, :, :], 0.0).then_inc(s_zero, 1)
            dve.memset(lastq[:, :, :], 0.0).then_inc(s_zero, 1)
            dve.wait_ge(s_w0, 16)
            for h, at in pair_runs():
                dve.tensor_tensor(pk[:, at:at + F - 1 - h], w0v[:, h, h + 1:F], w0v[:, h + 1:F, h], ALU.add)
            dve.tensor_reduce(rsum[:, 0, :], w0v, AX_X, ALU.add)
            dve.tensor_reduce(rsum[:, 1, :], w0v.rearrange("o h m -> o m h"), AX_X, ALU.add).then_inc(s_prep, 1)
            dve.wait_ge(s_prep, 1)
            dve.tensor_tensor(rsum[:, 2, :], rsum[:, 0, :], rsum[:, 1, :], ALU.add).then_inc(s_prep, 1)
            dve.wait_ge(s_prep, 2)
            dve.scalar_tensor_tensor(out=pk[:, NPAIR:NSQ], in0=w0s[:, 0:F * F:F + 1], scalar=4.0, in1=rsum[:, 2, :],
                                     op0=ALU.mult, op1=ALU.subtract).then_inc(s_prep, 1)
            dve.wait_ge(s_wsplit, 1)
            dve.tensor_tensor(w1l[:, :, :], w1v, w1h[:, :, :].bitcast(F32), ALU.subtract).then_inc(s_prep, 1)
            dve.wait_ge(s_wsplit, 2)
            dve.wait_ge(s_prep, 4)
            dve.wait_ge(s_zero, 5)
            dve.scalar_tensor_tensor(out=pkl[:, :], in0=pk[:, :], scalar=0.5, in1=pkh[:, :].bitcast(F32),
                                     op0=ALU.mult, op1=ALU.subtract).then_inc(s_prep, 1)
            dve.wait_ge(s_prep, 5)
            wh = w1h[:, F - 1, :].bitcast(F32)
            dve.tensor_copy(lastp[:, 0, 0:H0], wh)
            dve.tensor_copy(lastp[:, 0, H0:P], w1l[:, F - 1, :].bitcast(F32))
            dve.tensor_copy(lastp[:, 1, 0:H0], wh)
            qhr, qlr = pkh[:, Q_FULL * P:NSQ].bitcast(F32), pkl[:, Q_FULL * P:NSQ].bitcast(F32)
            dve.tensor_copy(lastq[:, 0, 0:Q_REST], qhr)
            dve.tensor_copy(lastq[:, 0, Q_REST:2 * Q_REST], qlr)
            dve.tensor_copy(lastq[:, 1, 0:Q_REST], qhr).then_inc(s_prep, 1)
            dve.wait_ge(s_small, 80)
            dve.tensor_scalar(nb0[:, :], bias0[:, :], -1.0, None, ALU.mult).then_inc(s_half0, 1)
            dve.tensor_scalar(nb1[:, :], bias1[:, :], -1.0, None, ALU.mult).then_inc(s_half1, 1)
            dve.tensor_scalar(db0[:, :], bias0[:, :], float(D), None, ALU.mult).then_inc(s_ht0, 1)
            dve.wait_ge(s_small, 80)
            dve.memset(tmp0[:, :], 0.0).then_inc(s_ht1, 1)
            dve.tensor_scalar(db1[:, :], bias1[:, :], float(D), None, ALU.mult).then_inc(s_bias, 1)
            for g in range(1, NG, 2):
                dve.wait_ge(s_turn, g + 1)
                for j, (_, dst) in enumerate(groups[g]):
                    last = dve.tensor_copy(dst, bb[:, g % NB, j * P:(j + 1) * P])
                last.then_inc(s_turned_v, 1)
            dve.wait_ge(s_turn, NG + 1)
            dve.tensor_copy(htb[0:DENSE, 0:2 * C], bb[0:DENSE, NG % NB, :]).then_inc(s_turned_v, 1)
            dve.wait_ge(s_turn, NG + 2)
            dve.tensor_copy(htb[0:DENSE, 2 * C:4 * C], bb[0:DENSE, (NG + 1) % NB, :]).then_inc(s_turned_v, 1)
            dve.wait_ge(s_bias, 1)
            for n, job in enumerate(HEAD):
                if job[0] == "q":
                    low(n, wide(job), n - 1)
            direct0(0, 0, 0, ZH_)
            slot(0, 0, 0, first=True)
            with dve.Fori(0, BT - 2) as b:
                for r in (1, 2, 3):
                    slot(b * G + r, b, r)
                slot(b * G + G, b + 1, 0)
            for t in range(NT - 7, NT):
                slot(t, t // G, t % G)
            direct1(NT - 1, BT - 1, 3, ZH_ + NT * ZJ - 4)
            finish(BT - 1, hi, acc1, tmp1, db1, hta, s_acc1, s_half1, s_ht1)

        @block.tensor
        def _(pe):
            def turn_x(i, g):
                for d in range(DG):
                    mm = pe.transpose(bb[0:KX, i % NB, d * H0:(d + 1) * H0].bitcast(BF16),
                                      xs[:, :, :, g * DG + d].rearrange("p a f -> p (a f)"), identb[:, :])
                mm.then_inc(s_bcast, 1)

            def broadcast(i, job, u):
                base = 0 if job[0] == "q" else NQ
                for j, c in enumerate(chunks(job)):
                    mm = pe.matmul(bb[:, i % NB, j * C:(j + 1) * C], sel[:, (base + c) * P:(base + c + 1) * P],
                                   xt[:, u, :], start=True, stop=True)
                mm.then_inc(s_bcast, 1)

            def weigh(i, job):
                y, wh, wl, count = (y0p, qh, ql, NQ) if job[0] == "q" else (y1p, ph, pl, NP1)
                for j, c in enumerate(chunks(job)):
                    cols = slice(j * C, (j + 1) * C)
                    high, low = zh[:, i % NZ, cols], zl[:, i % NZ, cols]
                    if c < count - 1:
                        pe.matmul(y[:, :], wh[:, c, :], high, start=(c == 0), stop=False)
                        pe.matmul(y[:, :], wl[:, c, :], high, start=False, stop=False)
                        mm = pe.matmul(y[:, :], wh[:, c, :], low, start=False, stop=False)
                    else:
                        pe.matmul(y[:, :], wh[:, c, :], high, start=False, stop=False)
                        mm = pe.matmul(y[:, :], wl[:, c, :], low, start=False, stop=True)
                mm.then_inc(s_main, 1)

            def wait_low(t, bt, r, n):
                if lo_on_pool(r, ORDER[n]):
                    pe.wait_ge(s_lop, lo_done(t, bt, r, n, True))
                else:
                    pe.wait_ge(s_lod, lo_done(t, bt, r, n, False))

            def slot(t, bt, r, first=False):
                for n, job in enumerate(ORDER):
                    i = JH + r * J + n
                    if exists(t, job[0]):
                        m, u = (n - NB, t) if n >= NB else (n - NB + J, t - 1)
                        kind = ORDER[m][0]
                        if first and n < NB:
                            pe.wait_ge(s_hi, ZH_ + n - NB + 1)
                        elif kind == "p":
                            pe.wait_ge(s_prod, prods_done(u, m))
                        elif kind == "q" and exists(u, kind):
                            pe.wait_ge(s_hi, hi_done(u, m))
                        elif kind == "x" and exists(u, kind):
                            pe.wait_ge(s_xt, u + 3)
                        if job[0] == "x":
                            if r == 2:
                                pe.wait_ge(s_part, bt * 3 + 6)
                            turn_x(i, (r + 2) % G)
                        else:
                            if n == QJ[0]:
                                pe.wait_ge(s_xt, t + 2)
                            broadcast(i, job, (r + 1) % 4 if job[0] == "q" else r)
                    if n < LAG and first:
                        continue
                    m, u = (n - LAG, t) if n >= LAG else (n - LAG + J, t - 1)
                    old = ORDER[m]
                    if old[0] == "x" or not exists(u, old[0]):
                        continue
                    if n >= LAG:
                        wait_low(t, bt, r, m)
                    else:
                        wait_low(t - 1, bt - 1 if r == 0 else bt, (r - 1) % G, m)
                    if old == ("q", 0):
                        pe.wait_ge(s_y2, t + 1)
                        pe.wait_ge(s_acc0, t + 1)
                    if old == ("p", 0) and not first:
                        pe.wait_ge(s_acc1, t)
                    weigh(i - LAG, old)

            def wait_turned(g):
                if g >= NG:
                    pe.wait_ge(s_turned_v, NG // 2 + 1 + g - NG)
                elif g % 2 == 0:
                    pe.wait_ge(s_turned_a, g // 2 + 1)
                else:
                    pe.wait_ge(s_turned_v, g // 2 + 1)

            pe.wait_ge(s_const, 48)
            for g, group in enumerate(groups):
                if g == 0:
                    pe.wait_ge(s_prep, 4)
                if g == 2 * (NP1 - 1) // TG:
                    pe.wait_ge(s_prep, 6)
                if g >= NB:
                    wait_turned(g - NB)
                for j, (src, _) in enumerate(group):
                    src = src if src.dtype == F32 else src.bitcast(F32)
                    mm = pe.transpose(bb[:, g % NB, j * P:(j + 1) * P], src, identf[:, :])
                mm.then_inc(s_turn, 1)
            pe.wait_ge(s_top, 80)
            for g in (NG, NG + 1):
                wait_turned(g - NB)
                for j in range(TG):
                    mm = pe.transpose(bb[0:DENSE, g % NB, j * P:(j + 1) * P], dn[:, (g - NG) * TG + j, :], identf[:, :])
                mm.then_inc(s_turn, 1)
            for g in range(NG + 2 - NB, NG + 2):
                wait_turned(g)
            pe.wait_ge(s_part, 3)
            for n, job in enumerate(HEAD):
                if n == 2:
                    pe.wait_ge(s_xt, 1)
                if n == 3 or n == 4:
                    pe.wait_ge(s_xt, n - 2)
                if n == 5:
                    pe.wait_ge(s_hi, 1)
                if job[0] == "x":
                    turn_x(n, job[1])
                else:
                    broadcast(n, job, 0)
            for n, job in enumerate(HEAD):
                if job[0] == "q":
                    pe.wait_ge(s_lod, n - 1)
                    weigh(n, job)
            slot(0, 0, 0, first=True)
            with pe.Fori(0, BT - 2) as b:
                for r in (1, 2, 3):
                    slot(b * G + r, b, r)
                slot(b * G + G, b + 1, 0)
            for t in range(NT - 7, NT):
                slot(t, t // G, t % G)
            for n in range(J - LAG, J):
                if ORDER[n][0] == "p":
                    wait_low(NT - 1, BT - 1, G - 1, n)
                    weigh(JH + 3 * J + n, ORDER[n])
            pe.wait_ge(s_ht0, BT + 1)
            pe.wait_ge(s_ht1, BT + 1)
            for g in range(G):
                cols = slice(g * C, (g + 1) * C)
                for k in range(N1 // P):
                    if k == NB:
                        pe.wait_ge(s_a1, g * (N1 // P) + 1)
                    elif g:
                        pe.wait_ge(s_a1, g * (N1 // P))
                    pe.matmul(bb[:, k % NB, 0:C], wa[:, k * P:(k + 1) * P], hta[:, cols], start=True, stop=False)
                    pe.matmul(bb[:, k % NB, 0:C], wb[:, k * P:(k + 1) * P], htb[:, cols], start=False, stop=True)\
                      .then_inc(s_m1, 1)
                for k in range(N2 // P):
                    pe.wait_ge(s_a1, (g + 1) * (N1 // P))
                    if g:
                        pe.wait_ge(s_a2, g * (N2 // P))
                    for c in range(N1 // P):
                        mm = pe.matmul(bb[:, k, C:2 * C], w2s[:, c, k * P:(k + 1) * P], h1[:, c, :],
                                       start=(c == 0), stop=(c == N1 // P - 1))
                    mm.then_inc(s_m2, 1)
                pe.wait_ge(s_a2, (g + 1) * (N2 // P))
                if g:
                    pe.wait_ge(s_a3, g)
                for c in range(N2 // P):
                    mm = pe.matmul(y0p[0:1, :], w3s[:, c:c + 1], h2[:, c, :], start=(c == 0), stop=(c == N2 // P - 1))
                mm.then_inc(s_m3, 1)


def kernel(**inputs):
    import concourse.bacc as bacc
    import ml_dtypes
    from concourse.bass_utils import run_bass_kernel_spmd

    nc = bacc.Bacc("TRN2", target_bir_lowering=False, num_devices=1)
    arrays = {}

    def given(name, a):
        a = np.ascontiguousarray(a)
        arrays[f"in_{name}"] = a
        return nc.dram_tensor(f"in_{name}", a.shape, mybir.dt.from_np(a.dtype), kind="ExternalInput").ap()

    aps = {name: given(name, inputs[name]) for name in inputs}
    sel = given("selections", selections().astype(ml_dtypes.bfloat16))
    identb = given("identity_bf16", np.eye(P, dtype=ml_dtypes.bfloat16))
    identf = given("identity_f32", np.eye(P, dtype=np.float32))
    out = nc.dram_tensor("out_0", (B, 1), F32, kind="ExternalOutput").ap()
    dlrm_cin_tower(nc, aps["dense_ctx"], aps["ids"], [aps[f"tbl_{f}"] for f in range(F)],
                   aps["W_top1"], aps["b_top1"], aps["W_top2"], aps["b_top2"], aps["W_top3"],
                   aps["L0_rec_W0"], aps["L0_rec_b0"], aps["L0_rec_W1"], aps["L0_rec_b1"],
                   sel, identb, identf, out)
    r = run_bass_kernel_spmd(nc, [arrays], core_ids=[0])
    return r.results[0]["out_0"]
```

```python
from contextlib import ExitStack

import numpy as np
import concourse.bass as bass
from concourse import mybir

F32 = mybir.dt.float32
F32R = mybir.dt.float32r
BF16 = mybir.dt.bfloat16
I32 = mybir.dt.int32
ALU = mybir.AluOpType
ACT = mybir.ActivationFunctionType
AX_X = mybir.AxisListType.X

B, F, D = 2048, 39, 16
P = 128
BT = B // P
DG = 4
G = D // DG
NT = BT * G
C = DG * P
MG = B // C
H0 = 64
PARTS = 3
KX = PARTS * F
NPAIR = F * (F - 1) // 2
NSQ = NPAIR + F
Q_FULL = NSQ // P
Q_REST = NSQ - Q_FULL * P
REST_ROWS = (0, 32, 64)
assert Q_REST <= 32
NQ = Q_FULL + 1
NP1 = (F + 1) // 2
N1, N2, DENSE = 512, 256, 16

ORDER = [('q', 0), ('q', 1), ('p', 0), ('p', 1), ('q', 2), ('p', 2), ('p', 3), ('q', 3), ('p', 4), ('p', 5), ('p', 6), ('x', 0), ('p', 7), ('p', 8), ('p', 9)]
HEAD = [("x", 0), ("x", 1), ("q", 0), ("q", 1), ("q", 2), ("q", 3)]
J, JH = len(ORDER), len(HEAD)
LAG = 4
NB = 3
NZ = 8
ZJ = J - 1
ZH_ = JH - 2
assert J * G % NB == 0 and ZJ * G % NZ == 0
QJ = [n for n, j in enumerate(ORDER) if j[0] == "q"]
PJ = [n for n, j in enumerate(ORDER) if j[0] == "p"]
XJ = ORDER.index(("x", 0))
PART_AT = [2, 5, 8]
REST_AT = [3, 6]
GATHER_AT = {2: [7, 8, 9, 10, 11, 12, 13, 14], 3: [0, 1, 2, 4, 5, 6, 8, 9, 10, 12, 13], 0: [0, 1, 3, 4, 6, 7, 9, 10, 12, 13], 1: [0, 1, 3, 4, 6, 7, 9, 10, 12, 13]}
assert GATHER_AT[2][0] > REST_AT[-1]
GATHER_FROM = {2: 0, 3: 8, 0: 19, 1: 29}
assert sum(len(x) for x in GATHER_AT.values()) == F
Y0_AT = QJ[-1] + LAG + 1
Y1_AT = LAG


WHOLE = [('p', 8), ('p', 9), ('p', 14), ('p', 15), ('q', 3), ('q', 0), ('q', 1), ('p', 12)]
NWH = len(WHOLE)
LAST_Q = ("q", NQ // 2)
assert ("q", NQ - 1) not in WHOLE and ("p", NP1 - 1) not in WHOLE


def chunks(job):
    kind, n = job
    return [NQ - 1] if job == LAST_Q else [2 * n, 2 * n + 1]


def split(job):
    at = [j for j, c in enumerate(chunks(job)) if (job[0], c) not in WHOLE]
    return slice(at[0] * C, (at[-1] + 1) * C) if at else None


def gathers_follow(t, bt, r):
    return not isinstance(t, int) or bt + (2 if r >= 2 else 1) < BT


def kind_count(kind, upto=J):
    return sum(1 for j in ORDER[:upto] if j[0] == kind)


def hi_count(upto=J):
    return sum(1 for j in ORDER[:upto] if j[0] == "q" or (j[0] == "p" and split(j)))


def lo_count(upto=J):
    return sum(1 for j in ORDER[:upto] if j[0] != "x" and split(j))


HEAD_LO = sum(1 for j in HEAD if j[0] == "q" and split(j))

def exists(t, kind):
    return not isinstance(t, int) or t < NT - {"p": 0, "q": 1, "x": 2}[kind]


def missing(t, n, kinds, chosen=lambda job: True):
    if not isinstance(t, int):
        return 0
    return sum(1 for u in range(NT - 2, t + 1) for j in ORDER[:n + 1 if u == t else J]
               if j[0] in kinds and not exists(u, j[0]) and chosen(j))


def bcast_done(t, n):
    if n < 0:
        return bcast_done(t - 1, n + J)
    return t * J + (JH + n + 1 - missing(t, n, "qx"))


def main_done(t, n):
    if n < 0:
        return main_done(t - 1, n + J)
    return t * ZJ + (ZH_ + n + 1 - kind_count("x", n + 1) - missing(t, n, "q"))


def prods_done(t, n):
    if n < 0:
        return prods_done(t - 1, n + J)
    return t * (NP1 // 2) + kind_count("p", n + 1)


def hi_done(t, n):
    return t * hi_count() + (ZH_ + hi_count(n + 1) - missing(t, n, "q"))


def lo_done(t, n):
    return t * lo_count() + (HEAD_LO + lo_count(n + 1) - missing(t, n, "q", split))


def z_slot(t, r, n):
    return (main_done(t if isinstance(t, int) else r, n) - 1) % NZ


def pair_runs():
    at, out = 0, []
    for h in range(F - 1):
        out.append((h, at))
        at += F - 1 - h
    return out


def selections():
    sel = np.zeros((F, (NQ + NP1) * P), np.float32)
    for h, at in pair_runs():
        for m in range(h + 1, F):
            sel[h, at + m - h - 1] = sel[m, at + m - h - 1] = 1
    for h in range(F):
        sel[h, NPAIR + h] = 1
    for at in REST_ROWS[1:]:
        sel[:, Q_FULL * P + at:Q_FULL * P + at + Q_REST] = sel[:, Q_FULL * P:NSQ]
    for k in range(NP1):
        for j in range(2):
            sel[min(2 * k + j, F - 1), (NQ + k) * P + j * H0:(NQ + k) * P + (j + 1) * H0] = 1
    return np.tile(sel, (PARTS, 1))


def dlrm_cin_tower(nc, dense, ids, tables, wt1, bt1, wt2, bt2, wt3, w0, b0, w1, b1,
                   sel_d, identb_d, identf_d, out):
    with ExitStack() as ctx:
        def sb(name, shape, dt, where=ctx):
            return where.enter_context(nc.sbuf_tensor(name, shape, dt))

        def sem(name):
            return ctx.enter_context(nc.semaphore(name))

        sel = sb("sel", [KX, (NQ + NP1) * P], BF16)
        identb = sb("identb", [P, P], BF16)
        identf = sb("identf", [P, P], F32)
        idx = sb("idx", [P, F], I32)
        xg = sb("xg", [P, F, D], F32)
        res1 = sb("res1", [P, F, D], F32)
        res2 = sb("res2", [P, F, D], F32)
        xs = sb("xs", [P, PARTS, F, D], BF16)
        xt = sb("xt", [KX, 4, C], BF16)
        y2 = sb("y2", [P, 2, C], F32)
        qh = sb("qh", [P, NQ, P], F32R)
        ql = sb("ql", [P, NQ - 1, P], F32R)
        ph = sb("ph", [P, NP1, P], F32R)
        pl = sb("pl", [P, NP1, P], F32R)
        w32 = sb("w32", [P, NWH, P], F32)
        acc0 = sb("acc0", [P, C], F32)
        acc1 = sb("acc1", [P, C], F32)
        tmp0 = sb("tmp0", [P, C // 2], F32)
        tmp1 = sb("tmp1", [P, C // 2], F32)
        bias0 = sb("bias0", [P, 1], F32)
        bias1 = sb("bias1", [P, 1], F32)
        nb0 = sb("nb0", [P, 1], F32)
        nb1 = sb("nb1", [P, 1], F32)
        db0 = sb("db0", [P, 1], F32)
        db1 = sb("db1", [P, 1], F32)
        hta = sb("hta", [P, B], F32)
        htb = sb("htb", [P, B], F32)
        t1h = sb("t1h", [P, 2, N1], F32R)
        t1l = sb("t1l", [P, 2, N1], F32R)
        t2h = sb("t2h", [P, N1 // P, N2], F32R)
        t2l = sb("t2l", [P, N1 // P, N2], F32R)
        w3s = sb("w3s", [P, N2 // P], F32)
        bt1s = sb("bt1s", [P, N1 // P], F32)
        bt2s = sb("bt2s", [P, N2 // P], F32)
        dn = sb("dn", [P, BT, DENSE], F32)
        with ExitStack() as scratch:
            w0s = sb("w0s", [P, F * F], F32, scratch)
            w1s = sb("w1s", [P, H0 * F], F32, scratch)
            pk = sb("pk", [P, NQ * P], F32, scratch)
            t1s = sb("t1s", [P, 2, N1], F32, scratch)
            t2s = sb("t2s", [P, N1 // P, N2], F32, scratch)
            rsum = sb("rsum", [P, 3, F], F32, scratch)
            pkh = sb("pkh", [P, NQ * P], F32R, scratch)
            pkl = sb("pkl", [P, NQ * P], F32R, scratch)
            w1h = sb("w1h", [P, F, H0], F32R, scratch)
            w1l = sb("w1l", [P, F, H0], F32R, scratch)
            stage = sb("stage", [P, NWH, P], F32, scratch)
            lastp = sb("lastp", [P, 2, P], F32, scratch)
            lastq = sb("lastq", [P, P], F32, scratch)
        with ExitStack() as after:
            hth = sb("hth", [P, 2, 2, C], F32R, after)
            htl = sb("htl", [P, 2, 2, C], F32R, after)
            h1 = sb("h1", [P, 2, C], F32, after)
            h1h = sb("h1h", [P, 2, N1 // P, C], F32R, after)
            h1l = sb("h1l", [P, 2, N1 // P, C], F32R, after)
            h2 = sb("h2", [P, 2, N2 // P, C], F32, after)
            ys = sb("ys", [1, B], F32, after)
        z = sb("z", [P, NZ, 2 * C], F32)
        zh = sb("zh", [P, NZ, 2 * C], F32R)
        zl = sb("zl", [P, NZ, 2 * C], F32R)

        bb = ctx.enter_context(nc.psum_tensor("bb", [P, NB, 2 * C], F32))
        y0p = ctx.enter_context(nc.psum_tensor("y0p", [P, C], F32))
        y1p = ctx.enter_context(nc.psum_tensor("y1p", [P, C], F32))

        s_w0 = sem("s_w0")
        s_w1 = sem("s_w1")
        s_const = sem("s_const")
        s_small = sem("s_small")
        s_top = sem("s_top")
        s_ids = sem("s_ids")
        s_gather = sem("s_gather")
        s_prep = sem("s_prep")
        s_wsplit = sem("s_wsplit")
        s_turn = sem("s_turn")
        s_turned_a = sem("s_turned_a")
        s_turned_v = sem("s_turned_v")
        s_zero = sem("s_zero")
        s_bias = sem("s_bias")
        s_part = sem("s_part")
        s_res = sem("s_res")
        s_bcast = sem("s_bcast")
        s_xt = sem("s_xt")
        s_prod = sem("s_prod")
        s_hi = sem("s_hi")
        s_lo = sem("s_lo")
        s_main = sem("s_main")
        s_y2 = sem("s_y2")
        s_acc0 = sem("s_acc0")
        s_acc1 = sem("s_acc1")
        s_half0 = sem("s_half0")
        s_half1 = sem("s_half1")
        s_ht0 = sem("s_ht0")
        s_ht1 = sem("s_ht1")
        s_m1 = sem("s_m1")
        s_m2 = sem("s_m2")
        s_m3 = sem("s_m3")
        s_th = sem("s_th")
        s_tl = sem("s_tl")
        s_l1 = sem("s_l1")
        s_a1 = sem("s_a1")
        s_a2 = sem("s_a2")
        s_a3 = sem("s_a3")
        s_out = sem("s_out")

        w1v = w1s[:, :].rearrange("o (h m) -> o m h", h=H0)
        w0v = w0s[:, :].rearrange("o (h m) -> o h m", h=F)
        turns = []
        for k in [k for k in range(NP1 - 1) if ("p", k) not in WHOLE]:
            turns += [(w1h[:, 2 * k:2 * k + 2, :].rearrange("o m h -> o (m h)"), ph[:, k, :]), (w1l[:, 2 * k:2 * k + 2, :].rearrange("o m h -> o (m h)"), pl[:, k, :])]
        later = len(turns)
        for c in [c for c in range(NQ - 1) if ("q", c) not in WHOLE]:
            turns += [(pkh[:, c * P:(c + 1) * P], qh[:, c, :]), (pkl[:, c * P:(c + 1) * P], ql[:, c, :])]
        turns += [(lastp[:, 0, :], ph[:, NP1 - 1, :]), (lastp[:, 1, :], pl[:, NP1 - 1, :]),
                  (lastq[:, :], qh[:, NQ - 1, :])]
        turns += [(stage[:, j, :], w32[:, j, :]) for j in range(NWH)]
        TG = 2 * C // P
        groups = [turns[i:i + TG] for i in range(0, len(turns), TG)]
        NG = len(groups)
        ND = BT // TG

        def top1_bank(n):
            return bb[:, n // 2 % 2, n % 2 * C:(n % 2 + 1) * C]

        def make_low(engine, job, k):
            cols = split(job)
            if job == LAST_Q:
                rows = slice(REST_ROWS[2], REST_ROWS[2] + 32)
                return engine.tensor_tensor(zh[rows, k, cols], z[rows, k, cols], zh[rows, k, cols].bitcast(F32),
                                            ALU.subtract)
            return engine.tensor_tensor(zl[:, k, cols], z[:, k, cols], zh[:, k, cols].bitcast(F32), ALU.subtract)

        block = ctx.enter_context(nc.Block())

        @block.sync
        def _(sp):
            sp.dma_start(idx[:, :], ids[0:P, :]).then_inc(s_ids, 16)
            sp.dma_start(w1s[:, :], w1).then_inc(s_w1, 16)
            sp.dma_start(w0s[:, :], w0).then_inc(s_w0, 16)
            sp.dma_start(identf[:, :], identf_d).then_inc(s_const, 16)
            sp.dma_start(identb[:, :], identb_d).then_inc(s_const, 16)
            sp.dma_start(sel[:, :], sel_d).then_inc(s_const, 16)
            sp.dma_start(bias0[:, :], b0.rearrange("(p a) -> p a", a=1)).then_inc(s_small, 16)
            sp.dma_start(bias1[:, :], b1.rearrange("(p a) -> p a", a=1)).then_inc(s_small, 16)
            sp.dma_start(bt1s[:, :], bt1.rearrange("(k p) -> p k", p=P),
                         allow_slow_non_contiguous=True).then_inc(s_small, 16)
            sp.dma_start(bt2s[:, :], bt2.rearrange("(k p) -> p k", p=P),
                         allow_slow_non_contiguous=True).then_inc(s_small, 16)
            sp.dma_start(w3s[:, :], wt3.rearrange("(k p) a -> p (k a)", p=P),
                         allow_slow_non_contiguous=True).then_inc(s_small, 16)
            sp.dma_start(dn[:, :, :], dense.rearrange("(t p) n -> p t n", p=P)).then_inc(s_top, 16)
            sp.dma_start(t1s[:, 0, :], wt1[H0:H0 + P, :]).then_inc(s_top, 16)
            sp.dma_start(t2s[:, :, :], wt2.rearrange("(k p) n -> p k n", p=P)).then_inc(s_top, 16)
            sp.wait_ge(s_zero, 2)
            sp.dma_start(t1s[H0:P, 1, :], wt1[0:H0, :]).then_inc(s_top, 16)
            sp.dma_start(t1s[0:DENSE, 1, :], wt1[H0 + P:H0 + P + DENSE, :]).then_inc(s_top, 16)
            with sp.Fori(1, BT) as b:
                sp.wait_ge(s_gather, b * (16 * F))
                sp.dma_start(idx[:, :], ids[bass.ts(b, P), :]).then_inc(s_ids, 16)
            sp.wait_ge(s_a3, MG)
            sp.dma_start(out.rearrange("b a -> a b"), ys[:, :]).then_inc(s_out, 16)
            sp.wait_ge(s_out, 16)

        @block.gpsimd
        def _(pool):
            def gather(f):
                pool.indirect_dma_start(xg[:, f, :], None, tables[f],
                                        bass.IndirectOffsetOnAxis(idx[:, f:f + 1], 0)).then_inc(s_gather, 16)

            def remainder(b, k, another):
                pool.wait_ge(s_part, b * 3 + k + 1)
                if k == 0:
                    pool.tensor_tensor(res1[:, :, :], xg[:, :, :], xs[:, 0, :, :], ALU.subtract).then_inc(s_res, 1)
                else:
                    pool.wait_ge(s_res, b * 2 + 1)
                    if another:
                        pool.wait_ge(s_ids, b * 16 + 32)
                    pool.tensor_tensor(res2[:, :, :], res1[:, :, :], xs[:, 1, :, :], ALU.subtract).then_inc(s_res, 1)

            def slot(t, bt, r):
                for n, job in enumerate(ORDER):
                    if n in GATHER_AT[r] and gathers_follow(t, bt, r):
                        gather(GATHER_FROM[r] + GATHER_AT[r].index(n))
                    if r == 2 and n in REST_AT and exists(t, "x"):
                        remainder(bt + 1, REST_AT.index(n), gathers_follow(t, bt, r))

            pool.wait_ge(s_ids, 16)
            for f in range(F):
                gather(f)
            pool.wait_ge(s_ids, 32)
            pool.wait_ge(s_res, 2)
            for f in range(GATHER_FROM[0]):
                gather(f)
            slot(0, 0, 0)
            with pool.Fori(0, BT - 2) as b:
                for r in (1, 2, 3):
                    slot(b * G + r, b, r)
                slot(b * G + G, b + 1, 0)
            for t in range(NT - 7, NT):
                slot(t, t // G, t % G)

        @block.scalar
        def _(act):
            def part(b, k, last_turn=None):
                if k == 0:
                    act.wait_ge(s_gather, b * (16 * F) + 16 * F)
                    if last_turn is not None:
                        act.wait_ge(s_bcast, last_turn)
                else:
                    act.wait_ge(s_res, b * 2 + k)
                act.activation(xs[:, k, :, :], (xg, res1, res2)[k][:, :, :], ACT.Copy).then_inc(s_part, 1)

            def take_xt(i, u, ready):
                act.wait_ge(s_bcast, ready)
                act.activation(xt[:, u, :], bb[0:KX, i % NB, 0:C // 2].bitcast(BF16), ACT.Copy)\
                   .then_inc(s_xt, 1)

            def squares(i, k, job, ready):
                w = len(chunks(job)) * C
                act.wait_ge(s_bcast, ready)
                last = act.activation(z[:, k, 0:w], bb[:, i % NB, 0:w], ACT.Square)
                if split(job):
                    last = act.activation(zh[:, k, split(job)], bb[:, i % NB, split(job)], ACT.Square)
                last.then_inc(s_hi, 1)

            def hidden(t, before, u):
                act.wait_ge(s_main, before)
                act.activation(y2[0:H0, u, :], y0p[0:H0, :], ACT.Relu, bias=bias0[0:H0, :])
                act.activation(y2[H0:P, u, :], y0p[0:H0, :], ACT.Relu, bias=bias0[0:H0, :]).then_inc(s_y2, 1)

            def slot(t, bt, r):
                first = isinstance(t, int) and t == 0
                for n, job in enumerate(ORDER):
                    i = JH + r * J + n
                    if job[0] == "x" and exists(t, "x"):
                        take_xt(i, (r + 2) % 4, bcast_done(t, n))
                    if job[0] == "q" and exists(t, "q"):
                        if not first or main_done(t, n) > NZ:
                            act.wait_ge(s_main, main_done(t, n) - NZ)
                        squares(i, z_slot(t, r, n), job, bcast_done(t, n))
                    if job[0] == "p" and split(job):
                        act.wait_ge(s_prod, prods_done(t, n))
                        k = z_slot(t, r, n)
                        act.activation(zh[:, k, split(job)], z[:, k, split(job)], ACT.Copy).then_inc(s_hi, 1)
                    if r == 2 and n in PART_AT and exists(t, "x"):
                        part(bt + 1, PART_AT.index(n), bcast_done(t, XJ - J))
                    if n == Y0_AT and exists(t, "q"):
                        act.wait_ge(s_prod, prods_done(t, -1))
                        hidden(t, main_done(t, QJ[-1]), (r + 1) % 2)

            act.wait_ge(s_w1, 16)
            act.activation(w1h[:, :, :], w1v, ACT.Copy).then_inc(s_wsplit, 1)
            act.wait_ge(s_prep, 3)
            act.activation(pkh[:, :], pk[:, :], ACT.Copy, scale=0.5).then_inc(s_wsplit, 1)
            for g in range(0, NG, 2):
                act.wait_ge(s_turn, g + 1)
                for j, (_, dst) in enumerate(groups[g]):
                    last = act.activation(dst, bb[:, g % NB, j * P:(j + 1) * P], ACT.Copy)
                last.then_inc(s_turned_a, 1)
            act.wait_ge(s_top, 80)
            act.activation(t1h[:, :, :], t1s[:, :, :], ACT.Copy)
            act.activation(t2h[:, :, :], t2s[:, :, :], ACT.Copy).then_inc(s_wsplit, 1)
            for k in range(PARTS):
                part(0, k)
            act.wait_ge(s_prep, 7)
            for n, job in enumerate(HEAD):
                if job[0] == "x":
                    take_xt(n, job[1], n + 1)
                else:
                    squares(n, n - 2, job, n + 1)
            hidden(-1, ZH_, 0)
            slot(0, 0, 0)
            with act.Fori(0, BT - 2) as b:
                for r in (1, 2, 3):
                    slot(b * G + r, b, r)
                slot(b * G + G, b + 1, 0)
            for t in range(NT - 7, NT):
                slot(t, t // G, t % G)
            def inputs_high(g):
                if g >= 2:
                    act.wait_ge(s_m1, (g - 1) * (N1 // P))
                act.activation(hth[:, g % 2, 0, :], hta[:, g * C:(g + 1) * C], ACT.Copy)
                act.activation(hth[:, g % 2, 1, :], htb[:, g * C:(g + 1) * C], ACT.Copy).then_inc(s_th, 1)

            def first(g):
                for k in range(N1 // P):
                    n = g * (N1 // P) + k
                    act.wait_ge(s_m1, n + 1)
                    if n >= 2:
                        act.wait_ge(s_l1, n - 1)
                    if g >= 2:
                        act.wait_ge(s_m2, (g - 1) * (N2 // P))
                    y = top1_bank(n)
                    act.activation(h1[:, n % 2, :], y, ACT.Relu, bias=bt1s[:, k:k + 1])
                    act.activation(h1h[:, g % 2, k, :], y, ACT.Relu, bias=bt1s[:, k:k + 1]).then_inc(s_a1, 1)

            def second(g):
                for k in range(N2 // P):
                    act.wait_ge(s_m2, g * (N2 // P) + k + 1)
                    if g >= 2:
                        act.wait_ge(s_m3, g - 1)
                    act.activation(h2[:, g % 2, k, :], bb[:, 2, k * C:(k + 1) * C], ACT.Relu, bias=bt2s[:, k:k + 1])\
                       .then_inc(s_a2, 1)

            def third(g):
                act.wait_ge(s_m3, g + 1)
                act.activation(ys[:, g * C:(g + 1) * C], (y0p, y1p)[g % 2][0:1, :], ACT.Copy).then_inc(s_a3, 1)

            act.wait_ge(s_ht0, BT + 1)
            act.wait_ge(s_ht1, BT + 1)
            inputs_high(0)
            inputs_high(1)
            first(0)
            for g in range(MG):
                if g + 2 < MG:
                    inputs_high(g + 2)
                if g + 1 < MG:
                    first(g + 1)
                second(g)
                if g >= 1:
                    third(g - 1)
            third(MG - 1)

        @block.vector
        def _(dve):
            def low(job, k, ready):
                dve.wait_ge(s_hi, ready)
                make_low(dve, job, k).then_inc(s_lo, 1)

            def direct0(u, bt, r, ready):
                dve.wait_ge(s_main, ready)
                y = y0p[H0:P, :]
                if r == 0:
                    if not (isinstance(u, int) and u == 0):
                        dve.wait_ge(s_half0, bt + 1)
                    dve.tensor_scalar(acc0[H0:P, :], y, nb0[H0:P, :], None, ALU.max).then_inc(s_acc0, 1)
                else:
                    dve.wait_ge(s_acc0, u)
                    dve.scalar_tensor_tensor(out=acc0[H0:P, :], in0=y, scalar=nb0[H0:P, :],
                                             in1=acc0[H0:P, :], op0=ALU.max, op1=ALU.add).then_inc(s_acc0, 1)

            def direct1(u, bt, r, ready):
                dve.wait_ge(s_main, ready)
                if r == 0:
                    if not (isinstance(u, int) and u == 0):
                        dve.wait_ge(s_half1, bt + 1)
                    dve.tensor_scalar(acc1[:, :], y1p[:, :], nb1[:, :], None, ALU.max).then_inc(s_acc1, 1)
                else:
                    dve.wait_ge(s_acc1, u)
                    dve.scalar_tensor_tensor(out=acc1[:, :], in0=y1p[:, :], scalar=nb1[:, :],
                                             in1=acc1[:, :], op0=ALU.max, op1=ALU.add).then_inc(s_acc1, 1)

            def finish(bt, rows, acc, tmp, db, ht, s_acc, s_half, s_ht):
                dve.wait_ge(s_acc, bt * G + G)
                dve.wait_ge(s_ht, bt + 1)
                dve.tensor_tensor(tmp[rows, :], acc[rows, 0:C // 2], acc[rows, C // 2:C], ALU.add).then_inc(s_half, 1)
                dve.wait_ge(s_half, bt + 2)
                dve.scalar_tensor_tensor(out=ht[rows, bass.ts(bt, P)], in0=tmp[rows, 0:P], scalar=db[rows, :],
                                         in1=tmp[rows, P:2 * P], op0=ALU.add, op1=ALU.add).then_inc(s_ht, 1)

            lo, hi = slice(H0, P), slice(0, P)

            def slot(t, bt, r):
                first = isinstance(t, int) and t == 0
                for n, job in enumerate(ORDER):
                    i = JH + r * J + n
                    if job[0] == "p":
                        dve.wait_ge(s_bcast, bcast_done(t, n))
                        if not first or main_done(t, n) > NZ:
                            dve.wait_ge(s_main, main_done(t, n) - NZ)
                        if job[1] == 0:
                            dve.wait_ge(s_y2, t + 1)
                        dve.tensor_tensor(z[:, z_slot(t, r, n), :].rearrange("p (k c) -> p k c", k=2),
                                          bb[:, i % NB, :].rearrange("p (k c) -> p k c", k=2),
                                          y2[:, r % 2, :].unsqueeze(1).to_broadcast([P, 2, C]),
                                          ALU.mult).then_inc(s_prod, 1)
                    if n > 0:
                        before = ORDER[n - 1]
                        if before[0] != "x" and exists(t, before[0]) and split(before):
                            low(before, z_slot(t, r, n - 1), hi_done(t, n - 1))
                    if n == J - 1 and job[0] != "x" and split(job):
                        low(job, z_slot(t, r, n), hi_done(t, n))
                    if n == Y1_AT and not first:
                        direct1(t - 1, bt, (r - 1) % G, main_done(t, -1))
                        if r == 0:
                            finish(bt - 1, hi, acc1, tmp1, db1, hta, s_acc1, s_half1, s_ht1)
                    if n == Y0_AT and exists(t, "q"):
                        direct0(t + 1, bt + 1 if r == 3 else bt, (r + 1) % G, main_done(t, QJ[-1]))
                        if r == 2:
                            finish(bt, lo, acc0, tmp0, db0, htb, s_acc0, s_half0, s_ht0)

            dve.memset(htb[0:H0, :], 0.0).then_inc(s_zero, 1)
            dve.memset(t1s[0:H0, 1, :], 0.0).then_inc(s_zero, 1)
            dve.memset(pk[:, NSQ:NQ * P], 0.0).then_inc(s_zero, 1)
            dve.memset(lastp[:, :, :], 0.0).then_inc(s_zero, 1)
            dve.memset(lastq[:, :], 0.0).then_inc(s_zero, 1)
            dve.wait_ge(s_w0, 16)
            for h, at in pair_runs():
                dve.tensor_tensor(pk[:, at:at + F - 1 - h], w0v[:, h, h + 1:F], w0v[:, h + 1:F, h], ALU.add)
            dve.tensor_reduce(rsum[:, 0, :], w0v, AX_X, ALU.add)
            dve.tensor_reduce(rsum[:, 1, :], w0v.rearrange("o h m -> o m h"), AX_X, ALU.add).then_inc(s_prep, 1)
            dve.wait_ge(s_prep, 1)
            dve.tensor_tensor(rsum[:, 2, :], rsum[:, 0, :], rsum[:, 1, :], ALU.add).then_inc(s_prep, 1)
            dve.wait_ge(s_prep, 2)
            dve.scalar_tensor_tensor(out=pk[:, NPAIR:NSQ], in0=w0s[:, 0:F * F:F + 1], scalar=4.0, in1=rsum[:, 2, :],
                                     op0=ALU.mult, op1=ALU.subtract).then_inc(s_prep, 1)
            dve.wait_ge(s_wsplit, 1)
            dve.tensor_tensor(w1l[:, :, :], w1v, w1h[:, :, :].bitcast(F32), ALU.subtract).then_inc(s_prep, 1)
            dve.wait_ge(s_wsplit, 2)
            dve.wait_ge(s_prep, 4)
            dve.wait_ge(s_zero, 5)
            dve.scalar_tensor_tensor(out=pkl[:, :], in0=pk[:, :], scalar=0.5, in1=pkh[:, :].bitcast(F32),
                                     op0=ALU.mult, op1=ALU.subtract).then_inc(s_prep, 1)
            dve.wait_ge(s_prep, 5)
            wh = w1h[:, F - 1, :].bitcast(F32)
            dve.tensor_copy(lastp[:, 0, 0:H0], wh)
            dve.tensor_copy(lastp[:, 0, H0:P], w1l[:, F - 1, :].bitcast(F32))
            dve.tensor_copy(lastp[:, 1, 0:H0], wh)
            qhr, qlr = pkh[:, Q_FULL * P:NSQ].bitcast(F32), pkl[:, Q_FULL * P:NSQ].bitcast(F32)
            for at, part in zip(REST_ROWS, (qhr, qlr, qhr)):
                dve.tensor_copy(lastq[:, at:at + Q_REST], part)
            for j, (kind, c) in enumerate(WHOLE):
                if kind == "p":
                    last = dve.tensor_copy(stage[:, j, :].rearrange("o (m h) -> o m h", m=2),
                                           w1v[:, 2 * c:2 * c + 2, :])
                else:
                    last = dve.tensor_scalar(stage[:, j, :], pk[:, c * P:(c + 1) * P], 0.5, None, ALU.mult)
            last.then_inc(s_prep, 1)
            dve.wait_ge(s_small, 80)
            dve.tensor_scalar(nb0[:, :], bias0[:, :], -1.0, None, ALU.mult).then_inc(s_half0, 1)
            dve.tensor_scalar(nb1[:, :], bias1[:, :], -1.0, None, ALU.mult).then_inc(s_half1, 1)
            dve.tensor_scalar(db0[:, :], bias0[:, :], float(D), None, ALU.mult).then_inc(s_ht0, 1)
            dve.wait_ge(s_small, 80)
            dve.memset(tmp0[:, :], 0.0).then_inc(s_ht1, 1)
            dve.tensor_scalar(db1[:, :], bias1[:, :], float(D), None, ALU.mult).then_inc(s_bias, 1)
            for g in range(1, NG, 2):
                dve.wait_ge(s_turn, g + 1)
                for j, (_, dst) in enumerate(groups[g]):
                    last = dve.tensor_copy(dst, bb[:, g % NB, j * P:(j + 1) * P])
                last.then_inc(s_turned_v, 1)
            for g in range(ND):
                dve.wait_ge(s_turn, NG + g + 1)
                dve.tensor_copy(htb[0:DENSE, 2 * C * g:2 * C * (g + 1)], bb[0:DENSE, (NG + g) % NB, :])\
                   .then_inc(s_turned_v, 1)
            dve.wait_ge(s_wsplit, 3)
            dve.tensor_tensor(t1l[:, :, :], t1s[:, :, :], t1h[:, :, :].bitcast(F32), ALU.subtract)
            dve.tensor_tensor(t2l[:, :, :], t2s[:, :, :], t2h[:, :, :].bitcast(F32), ALU.subtract).then_inc(s_prep, 1)
            dve.wait_ge(s_part, 1)
            dve.tensor_tensor(res1[:, :, :], xg[:, :, :], xs[:, 0, :, :], ALU.subtract).then_inc(s_res, 1)
            dve.wait_ge(s_part, 2)
            dve.wait_ge(s_res, 1)
            dve.tensor_tensor(res2[:, :, :], res1[:, :, :], xs[:, 1, :, :], ALU.subtract).then_inc(s_res, 1)
            dve.wait_ge(s_bias, 1)
            for n, job in enumerate(HEAD):
                if job[0] == "q" and split(job):
                    low(job, n - 2, n - 1)
            direct0(0, 0, 0, ZH_)
            slot(0, 0, 0)
            with dve.Fori(0, BT - 2) as b:
                for r in (1, 2, 3):
                    slot(b * G + r, b, r)
                slot(b * G + G, b + 1, 0)
            for t in range(NT - 7, NT):
                slot(t, t // G, t % G)
            direct1(NT - 1, BT - 1, 3, ZH_ + NT * ZJ - 4)
            finish(BT - 1, hi, acc1, tmp1, db1, hta, s_acc1, s_half1, s_ht1)

            def inputs_low(g):
                dve.wait_ge(s_th, g + 1)
                for k, ht in enumerate((hta, htb)):
                    last = dve.tensor_tensor(htl[:, g % 2, k, :], ht[:, g * C:(g + 1) * C],
                                             hth[:, g % 2, k, :].bitcast(F32), ALU.subtract)
                last.then_inc(s_tl, 1)

            def first_low(g):
                for k in range(N1 // P):
                    n = g * (N1 // P) + k
                    dve.wait_ge(s_a1, n + 1)
                    dve.tensor_tensor(h1l[:, g % 2, k, :], h1[:, n % 2, :], h1h[:, g % 2, k, :].bitcast(F32),
                                      ALU.subtract).then_inc(s_l1, 1)

            dve.wait_ge(s_ht1, BT + 1)
            inputs_low(0)
            inputs_low(1)
            first_low(0)
            for g in range(1, MG):
                if g + 1 < MG:
                    inputs_low(g + 1)
                first_low(g)

        @block.tensor
        def _(pe):
            def turn_x(i, g):
                for d in range(DG):
                    mm = pe.transpose(bb[0:KX, i % NB, d * H0:(d + 1) * H0].bitcast(BF16),
                                      xs[:, :, :, g * DG + d].rearrange("p a f -> p (a f)"), identb[:, :])
                mm.then_inc(s_bcast, 1)

            def broadcast(i, job, u):
                base = 0 if job[0] == "q" else NQ
                for j, c in enumerate(chunks(job)):
                    mm = pe.matmul(bb[:, i % NB, j * C:(j + 1) * C], sel[:, (base + c) * P:(base + c + 1) * P],
                                   xt[:, u, :], start=True, stop=True)
                mm.then_inc(s_bcast, 1)

            def weigh(i, job):
                y, wh, wl, count = (y0p, qh, ql, NQ) if job[0] == "q" else (y1p, ph, pl, NP1)
                for j, c in enumerate(chunks(job)):
                    cols = slice(j * C, (j + 1) * C)
                    if (job[0], c) in WHOLE:
                        mm = pe.matmul(y[:, :], w32[:, WHOLE.index((job[0], c)), :], z[:, i, cols],
                                       start=(c == 0), stop=False)
                        continue
                    high, low = zh[:, i, cols], zl[:, i, cols]
                    if c < count - 1:
                        pe.matmul(y[:, :], wh[:, c, :], high, start=(c == 0), stop=False)
                        pe.matmul(y[:, :], wl[:, c, :], high, start=False, stop=False)
                        mm = pe.matmul(y[:, :], wh[:, c, :], low, start=False, stop=False)
                    elif job == LAST_Q:
                        mm = pe.matmul(y[:, :], wh[:, c, :], high, start=False, stop=True)
                    else:
                        pe.matmul(y[:, :], wh[:, c, :], high, start=False, stop=False)
                        mm = pe.matmul(y[:, :], wl[:, c, :], low, start=False, stop=True)
                mm.then_inc(s_main, 1)

            def wait_z(t, n):
                if split(ORDER[n]):
                    pe.wait_ge(s_lo, lo_done(t, n))
                elif ORDER[n][0] == "p":
                    pe.wait_ge(s_prod, prods_done(t, n))
                else:
                    pe.wait_ge(s_hi, hi_done(t, n))

            def slot(t, bt, r):
                first = isinstance(t, int) and t == 0
                for n, job in enumerate(ORDER):
                    i = JH + r * J + n
                    if exists(t, job[0]):
                        m, u = (n - NB, t) if n >= NB else (n - NB + J, t - 1)
                        kind = ORDER[m][0]
                        if first and n < NB:
                            pe.wait_ge(s_hi, ZH_ + n - NB + 1)
                        elif kind == "p":
                            pe.wait_ge(s_prod, prods_done(u, m))
                        elif kind == "q" and exists(u, kind):
                            pe.wait_ge(s_hi, hi_done(u, m))
                        elif kind == "x" and exists(u, kind):
                            pe.wait_ge(s_xt, u + 3)
                        if job[0] == "x":
                            if r == 2:
                                pe.wait_ge(s_part, bt * 3 + 6)
                            turn_x(i, (r + 2) % G)
                        else:
                            if n == QJ[0]:
                                pe.wait_ge(s_xt, t + 2)
                            broadcast(i, job, (r + 1) % 4 if job[0] == "q" else r)
                    if n < LAG and first:
                        continue
                    m, u = (n - LAG, t) if n >= LAG else (n - LAG + J, t - 1)
                    old = ORDER[m]
                    if old[0] == "x" or not exists(u, old[0]):
                        continue
                    wait_z(u, m)
                    if old == ("q", 0):
                        pe.wait_ge(s_y2, t + 1)
                        pe.wait_ge(s_acc0, t + 1)
                    if old == ("p", 0) and not first:
                        pe.wait_ge(s_acc1, t)
                    weigh(z_slot(u, (r - 1) % G if n < LAG else r, m), old)

            def wait_turned(g):
                if g >= NG:
                    pe.wait_ge(s_turned_v, NG // 2 + 1 + g - NG)
                elif g % 2 == 0:
                    pe.wait_ge(s_turned_a, g // 2 + 1)
                else:
                    pe.wait_ge(s_turned_v, g // 2 + 1)

            pe.wait_ge(s_const, 48)
            for g, group in enumerate(groups):
                if g == 0:
                    pe.wait_ge(s_prep, 4)
                if g == later // TG:
                    pe.wait_ge(s_prep, 6)
                if g >= NB:
                    wait_turned(g - NB)
                for j, (src, _) in enumerate(group):
                    src = src if src.dtype == F32 else src.bitcast(F32)
                    mm = pe.transpose(bb[:, g % NB, j * P:(j + 1) * P], src, identf[:, :])
                mm.then_inc(s_turn, 1)
            pe.wait_ge(s_top, 80)
            for g in range(NG, NG + ND):
                wait_turned(g - NB)
                for j in range(TG):
                    mm = pe.transpose(bb[0:DENSE, g % NB, j * P:(j + 1) * P], dn[:, (g - NG) * TG + j, :], identf[:, :])
                mm.then_inc(s_turn, 1)
            for g in range(NG + ND - NB, NG + ND):
                wait_turned(g)
            pe.wait_ge(s_part, 3)
            for n, job in enumerate(HEAD):
                if n == 2:
                    pe.wait_ge(s_xt, 1)
                if n == 3 or n == 4:
                    pe.wait_ge(s_xt, n - 2)
                if n == 5:
                    pe.wait_ge(s_hi, 1)
                if job[0] == "x":
                    turn_x(n, job[1])
                else:
                    broadcast(n, job, 0)
            for n, job in enumerate(HEAD):
                if job[0] == "q":
                    if not split(job):
                        pe.wait_ge(s_hi, n - 1)
                    else:
                        pe.wait_ge(s_lo, sum(1 for j in HEAD[:n + 1] if j[0] == "q" and split(j)))
                    weigh(n - 2, job)
            slot(0, 0, 0)
            with pe.Fori(0, BT - 2) as b:
                for r in (1, 2, 3):
                    slot(b * G + r, b, r)
                slot(b * G + G, b + 1, 0)
            for t in range(NT - 7, NT):
                slot(t, t // G, t % G)
            for n in range(J - LAG, J):
                if ORDER[n][0] == "p":
                    wait_z(NT - 1, n)
                    weigh(z_slot(NT - 1, G - 1, n), ORDER[n])
            def top1(g):
                pe.wait_ge(s_tl, g + 1)
                for k in range(N1 // P):
                    n = g * (N1 // P) + k
                    if n >= 4:
                        pe.wait_ge(s_a1, n - 3)
                    y, m = top1_bank(n), slice(k * P, (k + 1) * P)
                    for j in range(2):
                        pe.matmul(y, t1h[:, j, m], hth[:, g % 2, j, :], start=(j == 0), stop=False)
                        pe.matmul(y, t1l[:, j, m], hth[:, g % 2, j, :], start=False, stop=False)
                        mm = pe.matmul(y, t1h[:, j, m], htl[:, g % 2, j, :], start=False, stop=(j == 1))
                    mm.then_inc(s_m1, 1)

            def top2(g):
                pe.wait_ge(s_l1, (g + 1) * (N1 // P))
                for k in range(N2 // P):
                    if g >= 1:
                        pe.wait_ge(s_a2, (g - 1) * (N2 // P) + k + 1)
                    y, m = bb[:, 2, k * C:(k + 1) * C], slice(k * P, (k + 1) * P)
                    for c in range(N1 // P):
                        pe.matmul(y, t2h[:, c, m], h1h[:, g % 2, c, :], start=(c == 0), stop=False)
                        pe.matmul(y, t2l[:, c, m], h1h[:, g % 2, c, :], start=False, stop=False)
                        mm = pe.matmul(y, t2h[:, c, m], h1l[:, g % 2, c, :], start=False, stop=(c == N1 // P - 1))
                    mm.then_inc(s_m2, 1)

            def top3(g):
                pe.wait_ge(s_a2, (g + 1) * (N2 // P))
                if g >= 2:
                    pe.wait_ge(s_a3, g - 1)
                for c in range(N2 // P):
                    mm = pe.matmul((y0p, y1p)[g % 2][0:1, :], w3s[:, c:c + 1], h2[:, g % 2, c, :],
                                   start=(c == 0), stop=(c == N2 // P - 1))
                mm.then_inc(s_m3, 1)

            pe.wait_ge(s_ht0, BT + 1)
            pe.wait_ge(s_ht1, BT + 1)
            top1(0)
            for g in range(MG):
                if g + 1 < MG:
                    top1(g + 1)
                top2(g)
                if g >= 1:
                    top3(g - 1)
            top3(MG - 1)


def kernel(**inputs):
    import concourse.bacc as bacc
    import ml_dtypes
    from concourse.bass_utils import run_bass_kernel_spmd

    nc = bacc.Bacc("TRN2", target_bir_lowering=False, num_devices=1)
    arrays = {}

    def given(name, a):
        a = np.ascontiguousarray(a)
        arrays[f"in_{name}"] = a
        return nc.dram_tensor(f"in_{name}", a.shape, mybir.dt.from_np(a.dtype), kind="ExternalInput").ap()

    aps = {name: given(name, inputs[name]) for name in inputs}
    sel = given("selections", selections().astype(ml_dtypes.bfloat16))
    identb = given("identity_bf16", np.eye(P, dtype=ml_dtypes.bfloat16))
    identf = given("identity_f32", np.eye(P, dtype=np.float32))
    out = nc.dram_tensor("out_0", (B, 1), F32, kind="ExternalOutput").ap()
    dlrm_cin_tower(nc, aps["dense_ctx"], aps["ids"], [aps[f"tbl_{f}"] for f in range(F)],
                   aps["W_top1"], aps["b_top1"], aps["W_top2"], aps["b_top2"], aps["W_top3"],
                   aps["L0_rec_W0"], aps["L0_rec_b0"], aps["L0_rec_W1"], aps["L0_rec_b1"],
                   sel, identb, identf, out)
    r = run_bass_kernel_spmd(nc, [arrays], core_ids=[0])
    return r.results[0]["out_0"]
```

```python
from contextlib import ExitStack

import numpy as np
import concourse.bass as bass
from concourse import mybir

F32 = mybir.dt.float32
F32R = mybir.dt.float32r
BF16 = mybir.dt.bfloat16
I32 = mybir.dt.int32
ALU = mybir.AluOpType
ACT = mybir.ActivationFunctionType
AX_X = mybir.AxisListType.X

B, F, D = 2048, 39, 16
P = 128
BT = B // P
DG = 4
G = D // DG
NT = BT * G
C = DG * P
MG = B // C
H0 = 64
COPIES = 8
PARTS = 3
KX = PARTS * F
NPAIR = F * (F - 1) // 2
NSQ = NPAIR + F
Q_FULL = NSQ // P
Q_REST = NSQ - Q_FULL * P
REST_ROWS = (0, 32, 64)
assert Q_REST <= 32
NQ = Q_FULL + 1
NP1 = (F + 1) // 2
N1, N2, DENSE = 512, 256, 16

ORDER = [("q", 0), ("q", 1), ("p", 0), ("p", 1), ("q", 2), ("p", 2), ("q", 3), ("p", 3), ("p", 4),
         ("p", 5), ("x", 0), ("p", 6), ("p", 7), ("p", 8), ("p", 9)]
HEAD = [("x", 0), ("x", 1), ("q", 0), ("q", 1), ("q", 2), ("q", 3)]
J, JH = len(ORDER), len(HEAD)
LAG = 4
NB = 3
NZ = 7
ZJ = J - 1
ZH_ = JH - 2
assert ZJ * G % NZ == 0
QJ = [n for n, j in enumerate(ORDER) if j[0] == "q"]
XJ = ORDER.index(("x", 0))
PART_AT = [3, 7, 8]
REST_AT = [6, 7]
SPREAD = [0, 1, 2, 3, 5, 6, 7, 8, 10, 11, 12, 13]
GATHER_AT = {2: [12, 13, 14], 3: SPREAD, 0: SPREAD, 1: SPREAD}
GATHER_FROM = {2: 0, 3: len(GATHER_AT[2]), 0: F - 2 * len(SPREAD), 1: F - len(SPREAD)}
assert GATHER_AT[2][0] > REST_AT[-1] and sum(len(x) for x in GATHER_AT.values()) == F
Y0_AT = QJ[-1] + LAG + 1
Y1_AT = LAG

WHOLE = [("q", 0), ("q", 1), ("p", 2), ("p", 3), ("p", 6), ("p", 7), ("p", 8), ("p", 9), ("p", 10),
         ("p", 11), ("p", 15)]
NWH = len(WHOLE)
LAST_Q = ("q", NQ // 2)
assert ("q", NQ - 1) not in WHOLE and ("p", NP1 - 1) not in WHOLE
SPLIT_Q = [c for c in range(NQ) if ("q", c) not in WHOLE]
SPLIT_P = [c for c in range(NP1) if ("p", c) not in WHOLE]


def chunks(job):
    kind, n = job
    return [NQ - 1] if job == LAST_Q else [2 * n, 2 * n + 1]


def split(job):
    at = [j for j, c in enumerate(chunks(job)) if (job[0], c) not in WHOLE]
    return slice(at[0] * C, (at[-1] + 1) * C) if at else None


LOADED = [("p", 2), ("p", 3), ("p", 4), ("p", 5), ("p", 6), ("p", 7)]
FL = 4 * LOADED[0][1]
NL = 4 * LOADED[-1][1] + 4 - FL
assert ("p", NP1 // 2 - 1) not in LOADED and len(LOADED) >= 4


def gathers_follow(t, bt, r):
    return not isinstance(t, int) or bt + (2 if r >= 2 else 1) < BT


def kind_count(kind, upto=J):
    return sum(1 for j in ORDER[:upto] if j[0] == kind)


def hi_count(upto=J):
    return sum(1 for j in ORDER[:upto] if j[0] == "q" or (j[0] == "p" and split(j)))


def lo_count(upto=J):
    return sum(1 for j in ORDER[:upto] if j[0] != "x" and split(j))


HEAD_LO = sum(1 for j in HEAD if j[0] == "q" and split(j))


def exists(t, kind):
    return kind == "p" or not isinstance(t, int) or t < NT - 1


def turns_follow(t):
    return not isinstance(t, int) or t < NT - 2


def missing(t, n, kinds, chosen=lambda job: True):
    if not isinstance(t, int):
        return 0
    return sum(1 for u in range(NT - 2, t + 1) for j in ORDER[:n + 1 if u == t else J]
               if j[0] in kinds and not exists(u, j[0]) and chosen(j))


def psum_count(upto=J):
    return sum(1 for j in ORDER[:upto] if j not in LOADED)


PSUM_AT = [n for n, j in enumerate(ORDER) if j not in LOADED]
JP = len(PSUM_AT)
assert JP * G % NB == 0


def bcast_done(t, n):
    if n < 0:
        return bcast_done(t - 1, n + J)
    return t * JP + (JH + psum_count(n + 1) - missing(t, n, "qx"))


def main_done(t, n):
    if n < 0:
        return main_done(t - 1, n + J)
    return t * ZJ + (ZH_ + n + 1 - kind_count("x", n + 1) - missing(t, n, "q"))


def prods_done(t, n):
    if n < 0:
        return prods_done(t - 1, n + J)
    return t * (NP1 // 2) + kind_count("p", n + 1)


def hi_done(t, n):
    return t * hi_count() + (ZH_ + hi_count(n + 1) - missing(t, n, "q"))


def lo_done(t, n):
    return t * lo_count() + (HEAD_LO + lo_count(n + 1) - missing(t, n, "q", split))


def z_slot(t, r, n):
    return (main_done(t if isinstance(t, int) else r, n) - 1) % NZ


def pair_runs():
    at, out = 0, []
    for h in range(F - 1):
        out.append((h, at))
        at += F - 1 - h
    return out


def selections():
    sel = np.zeros((F, (NQ + NP1) * P + NL), np.float32)
    sel[FL:FL + NL, (NQ + NP1) * P:] = np.eye(NL)
    for h, at in pair_runs():
        for m in range(h + 1, F):
            sel[h, at + m - h - 1] = sel[m, at + m - h - 1] = 1
    for h in range(F):
        sel[h, NPAIR + h] = 1
    for at in REST_ROWS[1:]:
        sel[:, Q_FULL * P + at:Q_FULL * P + at + Q_REST] = sel[:, Q_FULL * P:NSQ]
    for k in range(NP1):
        for j in range(2):
            sel[min(2 * k + j, F - 1), (NQ + k) * P + j * H0:(NQ + k) * P + (j + 1) * H0] = 1
    return np.tile(sel, (PARTS, 1))


def dlrm_cin_tower(nc, dense, ids, tables, wt1, bt1, wt2, bt2, wt3, w0, b0, w1, b1,
                   sel_d, identb_d, identf_d, xrows, out):
    with ExitStack() as ctx:
        def sb(name, shape, dt, where=ctx):
            return where.enter_context(nc.sbuf_tensor(name, shape, dt))

        def sem(name):
            return ctx.enter_context(nc.semaphore(name))

        sel = sb("sel", [KX, (NQ + NP1) * P + NL], BF16)
        identb = sb("identb", [P, P], BF16)
        identf = sb("identf", [P, P], F32)
        idx = sb("idx", [P, F], I32)
        xg = sb("xg", [P, F, D], F32)
        res1 = sb("res1", [P, F, D], F32)
        res2 = sb("res2", [P, F, D], F32)
        xs = sb("xs", [P, PARTS, F, D], BF16)
        xt = sb("xt", [KX, 4, C], BF16)
        xe = sb("xe", [NL, 2, C], F32)
        with ExitStack() as last:
            hth = sb("hth", [P, 2, 2, C], F32R, last)
            htl = sb("htl", [P, 2, 2, C], F32R, last)
        xb = sb("xb", [P, len(LOADED), 2, C], F32)
        y2 = sb("y2", [P, 2, C], F32)
        qh = sb("qh", [P, len(SPLIT_Q), P], F32R)
        ql = sb("ql", [P, len(SPLIT_Q) - 1, P], F32R)
        ph = sb("ph", [P, len(SPLIT_P), P], F32R)
        pl = sb("pl", [P, len(SPLIT_P), P], F32R)
        w32 = sb("w32", [P, NWH, P], F32)
        acc0 = sb("acc0", [P, C], F32)
        acc1 = sb("acc1", [P, C], F32)
        tmp0 = sb("tmp0", [P, C // 2], F32)
        tmp1 = sb("tmp1", [P, C // 2], F32)
        bias0 = sb("bias0", [P, 1], F32)
        bias1 = sb("bias1", [P, 1], F32)
        nb0 = sb("nb0", [P, 1], F32)
        nb1 = sb("nb1", [P, 1], F32)
        db0 = sb("db0", [P, 1], F32)
        db1 = sb("db1", [P, 1], F32)
        hta = sb("hta", [P, B], F32)
        htb = sb("htb", [P, B], F32)
        t1h = sb("t1h", [P, 2, N1], F32R)
        t1l = sb("t1l", [P, 2, N1], F32R)
        t2h = sb("t2h", [P, N1 // P, N2], F32R)
        t2l = sb("t2l", [P, N1 // P, N2], F32R)
        w3s = sb("w3s", [P, N2 // P], F32)
        bt1s = sb("bt1s", [P, N1 // P], F32)
        bt2s = sb("bt2s", [P, N2 // P], F32)
        dn = sb("dn", [P, BT, DENSE], F32)
        with ExitStack() as scratch:
            w0s = sb("w0s", [P, F * F], F32, scratch)
            w1s = sb("w1s", [P, H0 * F], F32, scratch)
            pk = sb("pk", [P, NQ * P], F32, scratch)
            t1s = sb("t1s", [P, 2, N1], F32, scratch)
            t2s = sb("t2s", [P, N1 // P, N2], F32, scratch)
            rsum = sb("rsum", [P, 3, F], F32, scratch)
            pkh = sb("pkh", [P, NQ * P], F32R, scratch)
            pkl = sb("pkl", [P, NQ * P], F32R, scratch)
            w1h = sb("w1h", [P, F, H0], F32R, scratch)
            w1l = sb("w1l", [P, F, H0], F32R, scratch)
            stage = sb("stage", [P, NWH, P], F32, scratch)
            lastp = sb("lastp", [P, 2, P], F32, scratch)
            lastq = sb("lastq", [P, P], F32, scratch)
        with ExitStack() as after:
            h1 = sb("h1", [P, 2, C], F32, after)
            h1h = sb("h1h", [P, 2, N1 // P, C], F32R, after)
            h1l = sb("h1l", [P, 2, N1 // P, C], F32R, after)
            h2 = sb("h2", [P, 2, N2 // P, C], F32, after)
            ys = sb("ys", [1, B], F32, after)
        z = sb("z", [P, NZ, 2 * C], F32)
        zh = sb("zh", [P, NZ, 2 * C], F32R)
        zl = sb("zl", [P, NZ, 2 * C], F32R)

        bb = ctx.enter_context(nc.psum_tensor("bb", [P, NB, 2 * C], F32))
        y0p = ctx.enter_context(nc.psum_tensor("y0p", [P, C], F32))
        y1p = ctx.enter_context(nc.psum_tensor("y1p", [P, C], F32))

        s_w0 = sem("s_w0")
        s_w1 = sem("s_w1")
        s_const = sem("s_const")
        s_small = sem("s_small")
        s_top = sem("s_top")
        s_ids = sem("s_ids")
        s_gather = sem("s_gather")
        s_prep = sem("s_prep")
        s_wsplit = sem("s_wsplit")
        s_turn = sem("s_turn")
        s_turned_a = sem("s_turned_a")
        s_turned_v = sem("s_turned_v")
        s_zero = sem("s_zero")
        s_bias = sem("s_bias")
        s_part = sem("s_part")
        s_res = sem("s_res")
        s_bcast = sem("s_bcast")
        s_xt = sem("s_xt")
        s_xe = sem("s_xe")
        s_saved = sem("s_saved")
        s_load = [sem(f"s_load{j}") for j in range(len(LOADED))]
        s_prod = sem("s_prod")
        s_hi = sem("s_hi")
        s_lo = sem("s_lo")
        s_main = sem("s_main")
        s_y2 = sem("s_y2")
        s_acc0 = sem("s_acc0")
        s_acc1 = sem("s_acc1")
        s_half0 = sem("s_half0")
        s_half1 = sem("s_half1")
        s_ht0 = sem("s_ht0")
        s_ht1 = sem("s_ht1")
        s_m1 = sem("s_m1")
        s_m2 = sem("s_m2")
        s_m3 = sem("s_m3")
        s_th = sem("s_th")
        s_tl = sem("s_tl")
        s_l1 = sem("s_l1")
        s_a1 = sem("s_a1")
        s_a2 = sem("s_a2")
        s_a3 = sem("s_a3")
        s_out = sem("s_out")

        w1v = w1s[:, :].rearrange("o (h m) -> o m h", h=H0)
        w0v = w0s[:, :].rearrange("o (h m) -> o h m", h=F)
        turns = []
        for k, c in enumerate(SPLIT_P[:-1]):
            turns += [(w1part[:, 2 * c:2 * c + 2, :].rearrange("o m h -> o (m h)"), kept[:, k, :])
                      for w1part, kept in ((w1h, ph), (w1l, pl))]
        later = len(turns)
        for k, c in enumerate(SPLIT_Q[:-1]):
            turns += [(pkh[:, c * P:(c + 1) * P], qh[:, k, :]), (pkl[:, c * P:(c + 1) * P], ql[:, k, :])]
        turns += [(lastp[:, 0, :], ph[:, len(SPLIT_P) - 1, :]), (lastp[:, 1, :], pl[:, len(SPLIT_P) - 1, :]),
                  (lastq[:, :], qh[:, len(SPLIT_Q) - 1, :])]
        turns += [(stage[:, j, :], w32[:, j, :]) for j in range(NWH)]
        TG = 2 * C // P
        groups = [turns[i:i + TG] for i in range(0, len(turns), TG)]
        NG = len(groups)
        ND = BT // TG

        def top1_bank(n):
            return bb[:, n // 2 % 2, n % 2 * C:(n % 2 + 1) * C]

        block = ctx.enter_context(nc.Block())

        @block.sync
        def _(sp):
            sp.dma_start(idx[:, :], ids[0:P, :]).then_inc(s_ids, 16)
            sp.dma_start(w1s[:, :], w1).then_inc(s_w1, 16)
            sp.dma_start(w0s[:, :], w0).then_inc(s_w0, 16)
            sp.dma_start(identf[:, :], identf_d).then_inc(s_const, 16)
            sp.dma_start(identb[:, :], identb_d).then_inc(s_const, 16)
            sp.dma_start(sel[:, :], sel_d).then_inc(s_const, 16)
            sp.dma_start(bias0[:, :], b0.rearrange("(p a) -> p a", a=1)).then_inc(s_small, 16)
            sp.dma_start(bias1[:, :], b1.rearrange("(p a) -> p a", a=1)).then_inc(s_small, 16)
            sp.dma_start(bt1s[:, :], bt1.rearrange("(k p) -> p k", p=P),
                         allow_slow_non_contiguous=True).then_inc(s_small, 16)
            sp.dma_start(bt2s[:, :], bt2.rearrange("(k p) -> p k", p=P),
                         allow_slow_non_contiguous=True).then_inc(s_small, 16)
            sp.dma_start(w3s[:, :], wt3.rearrange("(k p) a -> p (k a)", p=P),
                         allow_slow_non_contiguous=True).then_inc(s_small, 16)
            sp.dma_start(dn[:, :, :], dense.rearrange("(t p) n -> p t n", p=P)).then_inc(s_top, 16)
            sp.dma_start(t1s[:, 0, :], wt1[H0:H0 + P, :]).then_inc(s_top, 16)
            sp.dma_start(t2s[:, :, :], wt2.rearrange("(k p) n -> p k n", p=P)).then_inc(s_top, 16)
            sp.wait_ge(s_zero, 2)
            sp.dma_start(t1s[H0:P, 1, :], wt1[0:H0, :]).then_inc(s_top, 16)
            sp.dma_start(t1s[0:DENSE, 1, :], wt1[H0 + P:H0 + P + DENSE, :]).then_inc(s_top, 16)

            def save(u, ring):
                sp.wait_ge(s_xe, u + 1)
                sp.dma_start(xrows[bass.ds(u, 1), :, :, :].rearrange("a f r c -> (a f) r c"),
                             xe[:, ring, :].unsqueeze(1).to_broadcast([NL, COPIES, C]))\
                  .then_inc(s_saved, 16)
                sp.wait_ge(s_saved, u * 16 + 16)

            def load(u, j):
                f = 4 * LOADED[j][1] - FL
                for k in range(2):
                    rows = xrows[bass.ds(u, 1), f + 2 * k:f + 2 * k + 2, :, :].rearrange("a m r c -> (a m r) c")
                    sp.dma_start(xb[:, j, k, :], rows.unsqueeze(1).to_broadcast([2 * COPIES, H0 // COPIES, C]))\
                      .then_inc(s_load[j], 16)

            def slot(t, bt, r):
                if r == 2 and gathers_follow(t, bt, r):
                    sp.wait_ge(s_gather, bt * (16 * F) + 32 * F)
                    sp.dma_start(idx[:, :], ids[bass.ds(bt * P + 2 * P, P), :]).then_inc(s_ids, 16)
                save(t + 1, (r + 1) % 2)
                for j, job in enumerate(LOADED):
                    sp.wait_ge(s_prod, prods_done(t, ORDER.index(job)))
                    load(t + 1, j)

            sp.wait_ge(s_gather, 16 * F)
            sp.dma_start(idx[:, :], ids[P:2 * P, :]).then_inc(s_ids, 16)
            save(0, 0)
            for j in range(len(LOADED)):
                load(0, j)
            slot(0, 0, 0)
            with sp.Fori(0, BT - 2) as b:
                for r in (1, 2, 3):
                    slot(b * G + r, b, r)
                slot(b * G + G, b + 1, 0)
            for t in range(NT - 7, NT - 1):
                slot(t, t // G, t % G)
            sp.wait_ge(s_a3, MG)
            sp.dma_start(out.rearrange("b a -> a b"), ys[:, :]).then_inc(s_out, 16)
            sp.wait_ge(s_out, 16)

        @block.gpsimd
        def _(pool):
            def gather(f):
                pool.indirect_dma_start(xg[:, f, :], None, tables[f],
                                        bass.IndirectOffsetOnAxis(idx[:, f:f + 1], 0)).then_inc(s_gather, 16)

            def remainder(b, k, another):
                pool.wait_ge(s_part, b * 3 + k + 1)
                if k == 0:
                    pool.tensor_tensor(res1[:, :, :], xg[:, :, :], xs[:, 0, :, :], ALU.subtract).then_inc(s_res, 1)
                else:
                    pool.wait_ge(s_res, b * 2 + 1)
                    if another:
                        pool.wait_ge(s_ids, b * 16 + 32)
                    pool.tensor_tensor(res2[:, :, :], res1[:, :, :], xs[:, 1, :, :], ALU.subtract).then_inc(s_res, 1)

            def slot(t, bt, r):
                for n, job in enumerate(ORDER):
                    if n in GATHER_AT[r] and gathers_follow(t, bt, r):
                        gather(GATHER_FROM[r] + GATHER_AT[r].index(n))
                    if r == 2 and n in REST_AT and turns_follow(t):
                        remainder(bt + 1, REST_AT.index(n), gathers_follow(t, bt, r))

            pool.wait_ge(s_ids, 16)
            for f in range(F):
                gather(f)
            pool.wait_ge(s_ids, 32)
            pool.wait_ge(s_res, 2)
            for f in range(GATHER_FROM[0]):
                gather(f)
            slot(0, 0, 0)
            with pool.Fori(0, BT - 2) as b:
                for r in (1, 2, 3):
                    slot(b * G + r, b, r)
                slot(b * G + G, b + 1, 0)
            for t in range(NT - 7, NT):
                slot(t, t // G, t % G)

        @block.scalar
        def _(act):
            def part(b, k, last_turn=None):
                if k == 0:
                    act.wait_ge(s_gather, b * (16 * F) + 16 * F)
                    if last_turn is not None:
                        act.wait_ge(s_bcast, last_turn)
                else:
                    act.wait_ge(s_res, b * 2 + k)
                act.activation(xs[:, k, :, :], (xg, res1, res2)[k][:, :, :], ACT.Copy).then_inc(s_part, 1)

            def take_xt(i, u, ready):
                act.wait_ge(s_bcast, ready)
                act.activation(xt[:, u, :], bb[0:KX, i % NB, 0:C // 2].bitcast(BF16), ACT.Copy)\
                   .then_inc(s_xt, 1)

            def take_rows(i, u, ring, ready):
                act.wait_ge(s_bcast, ready)
                if not (isinstance(u, int) and u < 2):
                    act.wait_ge(s_saved, u * 16 - 16)
                act.activation(xe[:, ring, :], bb[0:NL, i % NB, C:2 * C], ACT.Copy).then_inc(s_xe, 1)

            def squares(i, k, job, ready):
                w = len(chunks(job)) * C
                act.wait_ge(s_bcast, ready)
                last = act.activation(z[:, k, 0:w], bb[:, i % NB, 0:w], ACT.Square)
                if split(job):
                    last = act.activation(zh[:, k, split(job)], bb[:, i % NB, split(job)], ACT.Square)
                last.then_inc(s_hi, 1)

            def hidden(t, before, u):
                act.wait_ge(s_main, before)
                act.activation(y2[0:H0, u, :], y0p[0:H0, :], ACT.Relu, bias=bias0[0:H0, :])
                act.activation(y2[H0:P, u, :], y0p[0:H0, :], ACT.Relu, bias=bias0[0:H0, :]).then_inc(s_y2, 1)

            def slot(t, bt, r):
                first = isinstance(t, int) and t == 0
                for n, job in enumerate(ORDER):
                    i = JH + r * JP + psum_count(n)
                    if job[0] == "x" and turns_follow(t):
                        take_xt(i, (r + 2) % 4, bcast_done(t, n))
                    if job[0] == "x" and exists(t, "x"):
                        take_rows(i, t + 1, (r + 1) % 2, bcast_done(t, n))
                    if job[0] == "q" and exists(t, "q"):
                        if not first or main_done(t, n) > NZ:
                            act.wait_ge(s_main, main_done(t, n) - NZ)
                        squares(i, z_slot(t, r, n), job, bcast_done(t, n))
                    if job[0] == "p" and split(job):
                        act.wait_ge(s_prod, prods_done(t, n))
                        k = z_slot(t, r, n)
                        act.activation(zh[:, k, split(job)], z[:, k, split(job)], ACT.Copy).then_inc(s_hi, 1)
                    if r == 2 and n in PART_AT and turns_follow(t):
                        part(bt + 1, PART_AT.index(n), bcast_done(t, XJ - J))
                    if n == Y0_AT and exists(t, "q"):
                        act.wait_ge(s_prod, prods_done(t, -1))
                        hidden(t, main_done(t, QJ[-1]), (r + 1) % 2)

            act.wait_ge(s_w1, 16)
            act.activation(w1h[:, :, :], w1v, ACT.Copy).then_inc(s_wsplit, 1)
            act.wait_ge(s_prep, 3)
            act.activation(pkh[:, :], pk[:, :], ACT.Copy, scale=0.5).then_inc(s_wsplit, 1)
            for g in range(0, NG, 2):
                act.wait_ge(s_turn, g + 1)
                for j, (_, dst) in enumerate(groups[g]):
                    last = act.activation(dst, bb[:, g % NB, j * P:(j + 1) * P], ACT.Copy)
                last.then_inc(s_turned_a, 1)
            act.wait_ge(s_top, 80)
            act.activation(t1h[:, :, :], t1s[:, :, :], ACT.Copy)
            act.activation(t2h[:, :, :], t2s[:, :, :], ACT.Copy).then_inc(s_wsplit, 1)
            for k in range(PARTS):
                part(0, k)
            act.wait_ge(s_prep, 7)
            for n, job in enumerate(HEAD):
                if job[0] == "x":
                    take_xt(n, job[1], n + 1)
                    if job[1] == 1:
                        take_rows(n, 0, 0, n + 1)
                else:
                    squares(n, n - 2, job, n + 1)
            hidden(-1, ZH_, 0)
            slot(0, 0, 0)
            with act.Fori(0, BT - 2) as b:
                for r in (1, 2, 3):
                    slot(b * G + r, b, r)
                slot(b * G + G, b + 1, 0)
            for t in range(NT - 7, NT):
                slot(t, t // G, t % G)
            def inputs_high(g):
                act.wait_ge(s_ht0, (g + 1) * (C // P) + 1)
                act.wait_ge(s_ht1, (g + 1) * (C // P) + 1)
                if g >= 2:
                    act.wait_ge(s_m1, (g - 1) * (N1 // P))
                act.activation(hth[:, g % 2, 0, :], hta[:, g * C:(g + 1) * C], ACT.Copy)
                act.activation(hth[:, g % 2, 1, :], htb[:, g * C:(g + 1) * C], ACT.Copy).then_inc(s_th, 1)

            def first(g):
                for k in range(N1 // P):
                    n = g * (N1 // P) + k
                    act.wait_ge(s_m1, n + 1)
                    if n >= 2:
                        act.wait_ge(s_l1, n - 1)
                    if g >= 2:
                        act.wait_ge(s_m2, (g - 1) * (N2 // P))
                    y = top1_bank(n)
                    act.activation(h1[:, n % 2, :], y, ACT.Relu, bias=bt1s[:, k:k + 1])
                    act.activation(h1h[:, g % 2, k, :], y, ACT.Relu, bias=bt1s[:, k:k + 1]).then_inc(s_a1, 1)

            def second(g):
                for k in range(N2 // P):
                    act.wait_ge(s_m2, g * (N2 // P) + k + 1)
                    if g >= 2:
                        act.wait_ge(s_m3, g - 1)
                    act.activation(h2[:, g % 2, k, :], bb[:, 2, k * C:(k + 1) * C], ACT.Relu, bias=bt2s[:, k:k + 1])\
                       .then_inc(s_a2, 1)

            def third(g):
                act.wait_ge(s_m3, g + 1)
                act.activation(ys[:, g * C:(g + 1) * C], (y0p, y1p)[g % 2][0:1, :], ACT.Copy).then_inc(s_a3, 1)

            act.wait_ge(s_prod, NT * (NP1 // 2))
            inputs_high(0)
            inputs_high(1)
            act.wait_ge(s_main, main_done(NT - 1, J - 1))
            first(0)
            for g in range(MG):
                if g + 2 < MG:
                    inputs_high(g + 2)
                if g + 1 < MG:
                    first(g + 1)
                second(g)
                if g >= 1:
                    third(g - 1)
            third(MG - 1)

        @block.vector
        def _(dve):
            def low(job, k, ready):
                cols = split(job)
                dve.wait_ge(s_hi, ready)
                if job == LAST_Q:
                    rows = slice(REST_ROWS[2], REST_ROWS[2] + 32)
                    dve.tensor_tensor(zh[rows, k, cols], z[rows, k, cols], zh[rows, k, cols].bitcast(F32),
                                      ALU.subtract).then_inc(s_lo, 1)
                else:
                    dve.tensor_tensor(zl[:, k, cols], z[:, k, cols], zh[:, k, cols].bitcast(F32),
                                      ALU.subtract).then_inc(s_lo, 1)

            def direct0(u, bt, r, ready):
                dve.wait_ge(s_main, ready)
                y = y0p[H0:P, :]
                if r == 0:
                    if not (isinstance(u, int) and u == 0):
                        dve.wait_ge(s_half0, bt + 1)
                    dve.tensor_scalar(acc0[H0:P, :], y, nb0[H0:P, :], None, ALU.max).then_inc(s_acc0, 1)
                else:
                    dve.wait_ge(s_acc0, u)
                    dve.scalar_tensor_tensor(out=acc0[H0:P, :], in0=y, scalar=nb0[H0:P, :],
                                             in1=acc0[H0:P, :], op0=ALU.max, op1=ALU.add).then_inc(s_acc0, 1)

            def direct1(u, bt, r, ready):
                dve.wait_ge(s_main, ready)
                if r == 0:
                    if not (isinstance(u, int) and u == 0):
                        dve.wait_ge(s_half1, bt + 1)
                    dve.tensor_scalar(acc1[:, :], y1p[:, :], nb1[:, :], None, ALU.max).then_inc(s_acc1, 1)
                else:
                    dve.wait_ge(s_acc1, u)
                    dve.scalar_tensor_tensor(out=acc1[:, :], in0=y1p[:, :], scalar=nb1[:, :],
                                             in1=acc1[:, :], op0=ALU.max, op1=ALU.add).then_inc(s_acc1, 1)

            def finish(bt, rows, acc, tmp, db, ht, s_acc, s_half, s_ht):
                dve.wait_ge(s_acc, bt * G + G)
                dve.wait_ge(s_ht, bt + 1)
                dve.tensor_tensor(tmp[rows, :], acc[rows, 0:C // 2], acc[rows, C // 2:C], ALU.add).then_inc(s_half, 1)
                dve.wait_ge(s_half, bt + 2)
                dve.scalar_tensor_tensor(out=ht[rows, bass.ts(bt, P)], in0=tmp[rows, 0:P], scalar=db[rows, :],
                                         in1=tmp[rows, P:2 * P], op0=ALU.add, op1=ALU.add).then_inc(s_ht, 1)

            lo, hi = slice(H0, P), slice(0, P)

            def slot(t, bt, r):
                first = isinstance(t, int) and t == 0
                for n, job in enumerate(ORDER):
                    i = JH + r * JP + psum_count(n)
                    if job[0] == "p":
                        if job in LOADED:
                            dve.wait_ge(s_load[LOADED.index(job)], t * 32 + 32)
                            copies = xb[:, LOADED.index(job), :, :]
                        else:
                            dve.wait_ge(s_bcast, bcast_done(t, n))
                            copies = bb[:, i % NB, :].rearrange("p (k c) -> p k c", k=2)
                        if not first or main_done(t, n) > NZ:
                            dve.wait_ge(s_main, main_done(t, n) - NZ)
                        if job[1] == 0:
                            dve.wait_ge(s_y2, t + 1)
                        dve.tensor_tensor(z[:, z_slot(t, r, n), :].rearrange("p (k c) -> p k c", k=2),
                                          copies, y2[:, r % 2, :].unsqueeze(1).to_broadcast([P, 2, C]),
                                          ALU.mult).then_inc(s_prod, 1)
                    if n > 0:
                        before = ORDER[n - 1]
                        if before[0] != "x" and exists(t, before[0]) and split(before):
                            low(before, z_slot(t, r, n - 1), hi_done(t, n - 1))
                    if n == J - 1 and job[0] != "x" and split(job):
                        low(job, z_slot(t, r, n), hi_done(t, n))
                    if n == Y1_AT and not first:
                        direct1(t - 1, bt, (r - 1) % G, main_done(t, -1))
                        if r == 0:
                            finish(bt - 1, hi, acc1, tmp1, db1, hta, s_acc1, s_half1, s_ht1)
                    if n == Y0_AT and exists(t, "q"):
                        direct0(t + 1, bt + 1 if r == 3 else bt, (r + 1) % G, main_done(t, QJ[-1]))
                        if r == 2:
                            finish(bt, lo, acc0, tmp0, db0, htb, s_acc0, s_half0, s_ht0)

            dve.memset(htb[0:H0, :], 0.0).then_inc(s_zero, 1)
            dve.memset(t1s[0:H0, 1, :], 0.0).then_inc(s_zero, 1)
            dve.memset(pk[:, NSQ:NQ * P], 0.0).then_inc(s_zero, 1)
            dve.memset(lastp[:, :, :], 0.0).then_inc(s_zero, 1)
            dve.memset(lastq[:, :], 0.0).then_inc(s_zero, 1)
            dve.wait_ge(s_w0, 16)
            for h, at in pair_runs():
                dve.tensor_tensor(pk[:, at:at + F - 1 - h], w0v[:, h, h + 1:F], w0v[:, h + 1:F, h], ALU.add)
            dve.tensor_reduce(rsum[:, 0, :], w0v, AX_X, ALU.add)
            dve.tensor_reduce(rsum[:, 1, :], w0v.rearrange("o h m -> o m h"), AX_X, ALU.add).then_inc(s_prep, 1)
            dve.wait_ge(s_prep, 1)
            dve.tensor_tensor(rsum[:, 2, :], rsum[:, 0, :], rsum[:, 1, :], ALU.add).then_inc(s_prep, 1)
            dve.wait_ge(s_prep, 2)
            dve.scalar_tensor_tensor(out=pk[:, NPAIR:NSQ], in0=w0s[:, 0:F * F:F + 1], scalar=4.0, in1=rsum[:, 2, :],
                                     op0=ALU.mult, op1=ALU.subtract).then_inc(s_prep, 1)
            dve.wait_ge(s_wsplit, 1)
            dve.tensor_tensor(w1l[:, :, :], w1v, w1h[:, :, :].bitcast(F32), ALU.subtract).then_inc(s_prep, 1)
            dve.wait_ge(s_wsplit, 2)
            dve.wait_ge(s_prep, 4)
            dve.wait_ge(s_zero, 5)
            dve.scalar_tensor_tensor(out=pkl[:, :], in0=pk[:, :], scalar=0.5, in1=pkh[:, :].bitcast(F32),
                                     op0=ALU.mult, op1=ALU.subtract).then_inc(s_prep, 1)
            dve.wait_ge(s_prep, 5)
            wh = w1h[:, F - 1, :].bitcast(F32)
            dve.tensor_copy(lastp[:, 0, 0:H0], wh)
            dve.tensor_copy(lastp[:, 0, H0:P], w1l[:, F - 1, :].bitcast(F32))
            dve.tensor_copy(lastp[:, 1, 0:H0], wh)
            qhr, qlr = pkh[:, Q_FULL * P:NSQ].bitcast(F32), pkl[:, Q_FULL * P:NSQ].bitcast(F32)
            for at, part in zip(REST_ROWS, (qhr, qlr, qhr)):
                dve.tensor_copy(lastq[:, at:at + Q_REST], part)
            for j, (kind, c) in enumerate(WHOLE):
                if kind == "p":
                    last = dve.tensor_copy(stage[:, j, :].rearrange("o (m h) -> o m h", m=2),
                                           w1v[:, 2 * c:2 * c + 2, :])
                else:
                    last = dve.tensor_scalar(stage[:, j, :], pk[:, c * P:(c + 1) * P], 0.5, None, ALU.mult)
            last.then_inc(s_prep, 1)
            dve.wait_ge(s_small, 80)
            dve.tensor_scalar(nb0[:, :], bias0[:, :], -1.0, None, ALU.mult).then_inc(s_half0, 1)
            dve.tensor_scalar(nb1[:, :], bias1[:, :], -1.0, None, ALU.mult).then_inc(s_half1, 1)
            dve.tensor_scalar(db0[:, :], bias0[:, :], float(D), None, ALU.mult).then_inc(s_ht0, 1)
            dve.wait_ge(s_small, 80)
            dve.memset(tmp0[:, :], 0.0).then_inc(s_ht1, 1)
            dve.tensor_scalar(db1[:, :], bias1[:, :], float(D), None, ALU.mult).then_inc(s_bias, 1)
            for g in range(1, NG, 2):
                dve.wait_ge(s_turn, g + 1)
                for j, (_, dst) in enumerate(groups[g]):
                    last = dve.tensor_copy(dst, bb[:, g % NB, j * P:(j + 1) * P])
                last.then_inc(s_turned_v, 1)
            for g in range(ND):
                dve.wait_ge(s_turn, NG + g + 1)
                dve.tensor_copy(htb[0:DENSE, 2 * C * g:2 * C * (g + 1)], bb[0:DENSE, (NG + g) % NB, :])\
                   .then_inc(s_turned_v, 1)
            dve.wait_ge(s_wsplit, 3)
            dve.tensor_tensor(t1l[:, :, :], t1s[:, :, :], t1h[:, :, :].bitcast(F32), ALU.subtract)
            dve.tensor_tensor(t2l[:, :, :], t2s[:, :, :], t2h[:, :, :].bitcast(F32), ALU.subtract).then_inc(s_prep, 1)
            dve.wait_ge(s_part, 1)
            dve.tensor_tensor(res1[:, :, :], xg[:, :, :], xs[:, 0, :, :], ALU.subtract).then_inc(s_res, 1)
            dve.wait_ge(s_part, 2)
            dve.wait_ge(s_res, 1)
            dve.tensor_tensor(res2[:, :, :], res1[:, :, :], xs[:, 1, :, :], ALU.subtract).then_inc(s_res, 1)
            dve.wait_ge(s_bias, 1)
            for n, job in enumerate(HEAD):
                if job[0] == "q" and split(job):
                    low(job, n - 2, n - 1)
            direct0(0, 0, 0, ZH_)
            slot(0, 0, 0)
            with dve.Fori(0, BT - 2) as b:
                for r in (1, 2, 3):
                    slot(b * G + r, b, r)
                slot(b * G + G, b + 1, 0)
            for t in range(NT - 7, NT):
                slot(t, t // G, t % G)
            def inputs_low(g):
                dve.wait_ge(s_th, g + 1)
                for k, ht in enumerate((hta, htb)):
                    last = dve.tensor_tensor(htl[:, g % 2, k, :], ht[:, g * C:(g + 1) * C],
                                             hth[:, g % 2, k, :].bitcast(F32), ALU.subtract)
                last.then_inc(s_tl, 1)

            def first_low(g):
                for k in range(N1 // P):
                    n = g * (N1 // P) + k
                    dve.wait_ge(s_a1, n + 1)
                    dve.tensor_tensor(h1l[:, g % 2, k, :], h1[:, n % 2, :], h1h[:, g % 2, k, :].bitcast(F32),
                                      ALU.subtract).then_inc(s_l1, 1)

            inputs_low(0)
            direct1(NT - 1, BT - 1, 3, main_done(NT - 1, J - 1))
            finish(BT - 1, hi, acc1, tmp1, db1, hta, s_acc1, s_half1, s_ht1)
            inputs_low(1)
            first_low(0)
            for g in range(1, MG):
                if g + 1 < MG:
                    inputs_low(g + 1)
                first_low(g)

        @block.tensor
        def _(pe):
            def turn_x(i, g):
                for d in range(DG):
                    mm = pe.transpose(bb[0:KX, i % NB, d * H0:(d + 1) * H0].bitcast(BF16),
                                      xs[:, :, :, g * DG + d].rearrange("p a f -> p (a f)"), identb[:, :])
                return mm

            def whole_rows(i, u):
                return pe.matmul(bb[0:NL, i % NB, C:2 * C], sel[:, (NQ + NP1) * P:(NQ + NP1) * P + NL], xt[:, u, :],
                                 start=True, stop=True)

            def broadcast(i, job, u):
                base = 0 if job[0] == "q" else NQ
                for j, c in enumerate(chunks(job)):
                    mm = pe.matmul(bb[:, i % NB, j * C:(j + 1) * C], sel[:, (base + c) * P:(base + c + 1) * P],
                                   xt[:, u, :], start=True, stop=True)
                mm.then_inc(s_bcast, 1)

            def weigh(i, job):
                y, wh, wl, kept = (y0p, qh, ql, SPLIT_Q) if job[0] == "q" else (y1p, ph, pl, SPLIT_P)
                for j, c in enumerate(chunks(job)):
                    cols = slice(j * C, (j + 1) * C)
                    if (job[0], c) in WHOLE:
                        mm = pe.matmul(y[:, :], w32[:, WHOLE.index((job[0], c)), :], z[:, i, cols],
                                       start=(c == 0), stop=False)
                        continue
                    high, low, k = zh[:, i, cols], zl[:, i, cols], kept.index(c)
                    if c != kept[-1]:
                        pe.matmul(y[:, :], wh[:, k, :], high, start=(c == 0), stop=False)
                        pe.matmul(y[:, :], wl[:, k, :], high, start=False, stop=False)
                        mm = pe.matmul(y[:, :], wh[:, k, :], low, start=False, stop=False)
                    elif job == LAST_Q:
                        mm = pe.matmul(y[:, :], wh[:, k, :], high, start=False, stop=True)
                    else:
                        pe.matmul(y[:, :], wh[:, k, :], high, start=False, stop=False)
                        mm = pe.matmul(y[:, :], wl[:, k, :], low, start=False, stop=True)
                mm.then_inc(s_main, 1)

            def wait_z(t, n):
                if split(ORDER[n]):
                    pe.wait_ge(s_lo, lo_done(t, n))
                elif ORDER[n][0] == "p":
                    pe.wait_ge(s_prod, prods_done(t, n))
                else:
                    pe.wait_ge(s_hi, hi_done(t, n))

            def slot(t, bt, r):
                first = isinstance(t, int) and t == 0
                for n, job in enumerate(ORDER):
                    i = JH + r * JP + psum_count(n)
                    if exists(t, job[0]) and job not in LOADED:
                        before = psum_count(n) - NB
                        m, u = PSUM_AT[before], (t if before >= 0 else t - 1)
                        kind = ORDER[m][0]
                        if first and before < 0:
                            pe.wait_ge(s_hi, ZH_ + before + 1)
                        elif kind == "p":
                            pe.wait_ge(s_prod, prods_done(u, m))
                        elif kind == "q" and exists(u, kind):
                            pe.wait_ge(s_hi, hi_done(u, m))
                        elif kind == "x" and exists(u, kind):
                            pe.wait_ge(s_xe, u + 2)
                        if job[0] == "x":
                            if r == 2 and turns_follow(t):
                                pe.wait_ge(s_part, bt * 3 + 6)
                            if turns_follow(t):
                                turn_x(i, (r + 2) % G)
                            pe.wait_ge(s_xt, t + 2)
                            whole_rows(i, (r + 1) % 4).then_inc(s_bcast, 1)
                        else:
                            if n == QJ[0]:
                                pe.wait_ge(s_xt, t + 2)
                            broadcast(i, job, (r + 1) % 4 if job[0] == "q" else r)
                    if n < LAG and first:
                        continue
                    m, u = (n - LAG, t) if n >= LAG else (n - LAG + J, t - 1)
                    old = ORDER[m]
                    if old[0] == "x" or not exists(u, old[0]):
                        continue
                    wait_z(u, m)
                    if old == ("q", 0):
                        pe.wait_ge(s_y2, t + 1)
                        pe.wait_ge(s_acc0, t + 1)
                    if old == ("p", 0) and not first:
                        pe.wait_ge(s_acc1, t)
                    weigh(z_slot(u, (r - 1) % G if n < LAG else r, m), old)

            def wait_turned(g):
                if g >= NG:
                    pe.wait_ge(s_turned_v, NG // 2 + 1 + g - NG)
                elif g % 2 == 0:
                    pe.wait_ge(s_turned_a, g // 2 + 1)
                else:
                    pe.wait_ge(s_turned_v, g // 2 + 1)

            pe.wait_ge(s_const, 48)
            for g, group in enumerate(groups):
                if g == 0:
                    pe.wait_ge(s_prep, 4)
                if g == later // TG:
                    pe.wait_ge(s_prep, 6)
                if g >= NB:
                    wait_turned(g - NB)
                for j, (src, _) in enumerate(group):
                    src = src if src.dtype == F32 else src.bitcast(F32)
                    mm = pe.transpose(bb[:, g % NB, j * P:(j + 1) * P], src, identf[:, :])
                mm.then_inc(s_turn, 1)
            pe.wait_ge(s_top, 80)
            for g in range(NG, NG + ND):
                wait_turned(g - NB)
                for j in range(TG):
                    mm = pe.transpose(bb[0:DENSE, g % NB, j * P:(j + 1) * P], dn[:, (g - NG) * TG + j, :], identf[:, :])
                mm.then_inc(s_turn, 1)
            for g in range(NG + ND - NB, NG + ND):
                wait_turned(g)
            pe.wait_ge(s_part, 3)
            for n, job in enumerate(HEAD):
                if n == 2:
                    pe.wait_ge(s_xt, 1)
                if n == 4:
                    pe.wait_ge(s_xe, 1)
                if n == 5:
                    pe.wait_ge(s_hi, 1)
                if job == ("x", 0):
                    turn_x(n, 0).then_inc(s_bcast, 1)
                elif job[0] == "x":
                    turn_x(n, 1)
                    pe.wait_ge(s_xt, 1)
                    whole_rows(n, 0).then_inc(s_bcast, 1)
                else:
                    broadcast(n, job, 0)
            for n, job in enumerate(HEAD):
                if job[0] == "q":
                    if not split(job):
                        pe.wait_ge(s_hi, n - 1)
                    else:
                        pe.wait_ge(s_lo, sum(1 for j in HEAD[:n + 1] if j[0] == "q" and split(j)))
                    weigh(n - 2, job)
            slot(0, 0, 0)
            with pe.Fori(0, BT - 2) as b:
                for r in (1, 2, 3):
                    slot(b * G + r, b, r)
                slot(b * G + G, b + 1, 0)
            for t in range(NT - 7, NT):
                slot(t, t // G, t % G)
            for n in range(J - LAG, J):
                if ORDER[n][0] == "p":
                    wait_z(NT - 1, n)
                    weigh(z_slot(NT - 1, G - 1, n), ORDER[n])
            def top1(g):
                pe.wait_ge(s_tl, g + 1)
                for k in range(N1 // P):
                    n = g * (N1 // P) + k
                    if n >= 4:
                        pe.wait_ge(s_a1, n - 3)
                    y, m = top1_bank(n), slice(k * P, (k + 1) * P)
                    for j in range(2):
                        pe.matmul(y, t1h[:, j, m], hth[:, g % 2, j, :], start=(j == 0), stop=False)
                        pe.matmul(y, t1l[:, j, m], hth[:, g % 2, j, :], start=False, stop=False)
                        mm = pe.matmul(y, t1h[:, j, m], htl[:, g % 2, j, :], start=False, stop=(j == 1))
                    mm.then_inc(s_m1, 1)

            def top2(g):
                pe.wait_ge(s_l1, (g + 1) * (N1 // P))
                for k in range(N2 // P):
                    if g >= 1:
                        pe.wait_ge(s_a2, (g - 1) * (N2 // P) + k + 1)
                    y, m = bb[:, 2, k * C:(k + 1) * C], slice(k * P, (k + 1) * P)
                    for c in range(N1 // P):
                        pe.matmul(y, t2h[:, c, m], h1h[:, g % 2, c, :], start=(c == 0), stop=False)
                        pe.matmul(y, t2l[:, c, m], h1h[:, g % 2, c, :], start=False, stop=False)
                        mm = pe.matmul(y, t2h[:, c, m], h1l[:, g % 2, c, :], start=False, stop=(c == N1 // P - 1))
                    mm.then_inc(s_m2, 1)

            def top3(g):
                pe.wait_ge(s_a2, (g + 1) * (N2 // P))
                if g >= 2:
                    pe.wait_ge(s_a3, g - 1)
                for c in range(N2 // P):
                    mm = pe.matmul((y0p, y1p)[g % 2][0:1, :], w3s[:, c:c + 1], h2[:, g % 2, c, :],
                                   start=(c == 0), stop=(c == N2 // P - 1))
                mm.then_inc(s_m3, 1)

            top1(0)
            for g in range(MG):
                if g + 1 < MG:
                    top1(g + 1)
                top2(g)
                if g == 1:
                    pe.wait_ge(s_ht0, BT + 1)
                    pe.wait_ge(s_ht1, BT + 1)
                if g >= 1:
                    top3(g - 1)
            top3(MG - 1)


def kernel(**inputs):
    import concourse.bacc as bacc
    import ml_dtypes
    from concourse.bass_utils import run_bass_kernel_spmd

    nc = bacc.Bacc("TRN2", target_bir_lowering=False, num_devices=1)
    arrays = {}

    def given(name, a):
        a = np.ascontiguousarray(a)
        arrays[f"in_{name}"] = a
        return nc.dram_tensor(f"in_{name}", a.shape, mybir.dt.from_np(a.dtype), kind="ExternalInput").ap()

    aps = {name: given(name, inputs[name]) for name in inputs}
    sel = given("selections", selections().astype(ml_dtypes.bfloat16))
    identb = given("identity_bf16", np.eye(P, dtype=ml_dtypes.bfloat16))
    identf = given("identity_f32", np.eye(P, dtype=np.float32))
    xrows = nc.dram_tensor("feature_rows", (NT, NL, COPIES, C), F32, kind="Internal").ap()
    out = nc.dram_tensor("out_0", (B, 1), F32, kind="ExternalOutput").ap()
    dlrm_cin_tower(nc, aps["dense_ctx"], aps["ids"], [aps[f"tbl_{f}"] for f in range(F)],
                   aps["W_top1"], aps["b_top1"], aps["W_top2"], aps["b_top2"], aps["W_top3"],
                   aps["L0_rec_W0"], aps["L0_rec_b0"], aps["L0_rec_W1"], aps["L0_rec_b1"],
                   sel, identb, identf, xrows, out)
    r = run_bass_kernel_spmd(nc, [arrays], core_ids=[0])
    return r.results[0]["out_0"]
```
